# Optimizing a Trainium2 kernel written in Bass

```python
import numpy as np
import jax
import jax.numpy as jnp

def _softmax(x, axis=-1):
    return jax.nn.softmax(x, axis=axis)

def _gelu(x):
    return jax.nn.gelu(x, approximate=True)

def _silu(x):
    return jax.nn.silu(x)

def _sigmoid(x):
    return jax.nn.sigmoid(x)

def _layernorm(x, axis=-1, eps=1e-05):
    m = jnp.mean(x, axis=axis, keepdims=True)
    v = jnp.var(x, axis=axis, keepdims=True)
    return (x - m) / jnp.sqrt(v + eps)

def _scatter_add(tgt, idx, src, axis=0):
    return tgt.at[idx].add(src)

def _segment_sum(src, seg, n):
    return jax.ops.segment_sum(src, seg, n)
kernel_name = 'mk_prb_d1_jaxref_r8_1023d4'

def setup_inputs(seed: int=0):
    np.random.seed(seed)
    _w = jnp.asarray

    def _L0_attn_setup():
        import jax, jax.numpy as jnp
        import numpy as np
        LAMBDA_0 = 1.0
        EPS = 1e-06
        key = jax.random.key(seed)
        ks = jax.random.split(key, 5)
        B, T, D, H = (4, 256, 128, 128)
        x = jax.random.normal(ks[0], (B, T, D), dtype=jnp.float32)
        Wq = jax.random.normal(ks[1], (H, D), dtype=jnp.float32) * D ** (-0.5)
        Wk = jax.random.normal(ks[2], (H, D), dtype=jnp.float32) * D ** (-0.5)
        Wv = jax.random.normal(ks[3], (H, D), dtype=jnp.float32) * D ** (-0.5)
        Wo = jax.random.normal(ks[4], (D, H), dtype=jnp.float32) * H ** (-0.5)
        bq = jnp.zeros((H,), jnp.float32)
        bk = jnp.zeros((H,), jnp.float32)
        bv = jnp.zeros((H,), jnp.float32)
        bo = jnp.zeros((D,), jnp.float32)
        return {'x': x, 'Wq': Wq, 'bq': bq, 'Wk': Wk, 'bk': bk, 'Wv': Wv, 'bv': bv, 'Wo': Wo, 'bo': bo}
    _L0_attn_in = _L0_attn_setup()

    def _L0_ffn_setup():
        import jax, jax.numpy as jnp
        import numpy as np
        B, S, D = (2, 256, 128)
        H, E, P, K = (8, 8, 128, 2)
        SCALE = 1.0 / np.sqrt(P)

        def _get_sel_gate(x, w, route_scale):
            logits = jnp.einsum('bsd,ed->bse', x, w).astype(jnp.float32)
            raw = logits.reshape(x.shape[0], x.shape[1], H, E)
            probs = jax.nn.sigmoid(raw)
            vals, idx = jax.lax.top_k(probs, K)
            vals = vals / jnp.clip(vals.sum(-1, keepdims=True), 1e-09)
            vals = vals * route_scale
            gate = (jax.nn.one_hot(idx, E, dtype=vals.dtype) * vals[..., None]).sum(-2)
            return gate
        key = jax.random.key(seed)
        ks = jax.random.split(key, 8)
        std = 1.0 / np.sqrt(D)
        return {'x': jax.random.normal(ks[0], (B, S, D), jnp.float32), 'q_w': jax.random.normal(ks[1], (H * P, D), jnp.float32) * std, 'k_w': jax.random.normal(ks[2], (H * P, D), jnp.float32) * std, 'v_w': jax.random.normal(ks[3], (H * E, D, P), jnp.float32) * std, 'o_w': jax.random.normal(ks[4], (H * E, P, D), jnp.float32) * (1.0 / np.sqrt(H * P)), 'sel_v_w': jax.random.normal(ks[5], (H * E, D), jnp.float32) * std, 'sel_o_w': jax.random.normal(ks[6], (H * E, D), jnp.float32) * std, 'route_scale': jnp.ones((1,), jnp.float32)}
    _L0_ffn_in = _L0_ffn_setup()
    _d = {'L0_attn_x': _L0_attn_in['x'], 'L0_attn_Wq': _L0_attn_in['Wq'], 'L0_attn_bq': _L0_attn_in['bq'], 'L0_attn_Wk': _L0_attn_in['Wk'], 'L0_attn_bk': _L0_attn_in['bk'], 'L0_attn_Wv': _L0_attn_in['Wv'], 'L0_attn_bv': _L0_attn_in['bv'], 'L0_attn_Wo': _L0_attn_in['Wo'], 'L0_attn_bo': _L0_attn_in['bo'], 'L0_ffn_q_w': _L0_ffn_in['q_w'], 'L0_ffn_k_w': _L0_ffn_in['k_w'], 'L0_ffn_v_w': _L0_ffn_in['v_w'], 'L0_ffn_o_w': _L0_ffn_in['o_w'], 'L0_ffn_sel_v_w': _L0_ffn_in['sel_v_w'], 'L0_ffn_sel_o_w': _L0_ffn_in['sel_o_w'], 'L0_ffn_route_scale': _L0_ffn_in['route_scale']}
    _x0 = _d['L0_attn_x']
    _d['L0_attn_x'] = jax.random.normal(jax.random.fold_in(jax.random.key(seed), 1), (4, 512, 128), dtype=_x0.dtype)
    del _x0
    return _d

def reference(L0_attn_x, L0_attn_Wq, L0_attn_bq, L0_attn_Wk, L0_attn_bk, L0_attn_Wv, L0_attn_bv, L0_attn_Wo, L0_attn_bo, L0_ffn_q_w, L0_ffn_k_w, L0_ffn_v_w, L0_ffn_o_w, L0_ffn_sel_v_w, L0_ffn_sel_o_w, L0_ffn_route_scale):

    def _L0_attn_ref(x, Wq, bq, Wk, bk, Wv, bv, Wo, bo):
        import jax, jax.numpy as jnp
        import numpy as np
        LAMBDA_0 = 1.0
        EPS = 1e-06
        B, T, D = x.shape
        H = Wq.shape[0]
        Q = jnp.einsum('btd,hd->bth', x, Wq) + bq
        K = jnp.einsum('btd,hd->bth', x, Wk) + bk
        V = jnp.einsum('btd,hd->bth', x, Wv) + bv
        A0 = jnp.broadcast_to(jnp.eye(H, dtype=jnp.float32) / LAMBDA_0, (B, H, H))
        M0 = jnp.zeros((B, H, H), jnp.float32)

        def step(carry, qkv):
            A, M = carry
            q, k, v = qkv
            s_t = jnp.sum(k * q, axis=-1, keepdims=True)
            u = k / (jnp.linalg.norm(k, axis=-1, keepdims=True) + EPS)
            Au = jnp.einsum('bij,bj->bi', A, u)
            denom = 1.0 + jnp.sum(u * Au, axis=-1, keepdims=True)
            A = A - jnp.einsum('bi,bj->bij', Au, Au) / denom[..., None]
            z = Au / denom
            alpha = s_t * z
            M = M + jnp.einsum('bi,bj->bij', v, alpha)
            o = jnp.einsum('bij,bj->bi', M, q)
            return ((A, M), o)
        qkv = (jnp.swapaxes(Q, 0, 1), jnp.swapaxes(K, 0, 1), jnp.swapaxes(V, 0, 1))
        _, O = jax.lax.scan(step, (A0, M0), qkv)
        O = jnp.swapaxes(O, 0, 1)
        return jnp.einsum('bth,dh->btd', O, Wo) + bo

    def _L0_ffn_ref(x, q_w, k_w, v_w, o_w, sel_v_w, sel_o_w, route_scale):
        import jax, jax.numpy as jnp
        import numpy as np
        B, S, D = (2, 256, 128)
        H, E, P, K = (8, 8, 128, 2)
        SCALE = 1.0 / np.sqrt(P)

        def _get_sel_gate(x, w, route_scale):
            logits = jnp.einsum('bsd,ed->bse', x, w).astype(jnp.float32)
            raw = logits.reshape(x.shape[0], x.shape[1], H, E)
            probs = jax.nn.sigmoid(raw)
            vals, idx = jax.lax.top_k(probs, K)
            vals = vals / jnp.clip(vals.sum(-1, keepdims=True), 1e-09)
            vals = vals * route_scale
            gate = (jax.nn.one_hot(idx, E, dtype=vals.dtype) * vals[..., None]).sum(-2)
            return gate
        rs = route_scale[0]
        gate_v = _get_sel_gate(x, sel_v_w, rs)
        gate_o = _get_sel_gate(x, sel_o_w, rs)
        q = jnp.einsum('bsd,hpd->bhsp', x, q_w.reshape(H, P, D))
        k = jnp.einsum('bsd,hpd->bhsp', x, k_w.reshape(H, P, D))
        xv = jnp.einsum('bsd,hedp->bshep', x, v_w.reshape(H, E, D, P))
        v = jnp.einsum('bshep,bshe->bhsp', xv, gate_v)
        att = jax.nn.softmax(jnp.einsum('bhqp,bhkp->bhqk', q, k) * SCALE, axis=-1)
        ctx = jnp.einsum('bhqk,bhkp->bqhp', att, v)
        weighted = ctx[:, :, :, None, :] * gate_o[..., None]
        out = jnp.einsum('bshep,hepd->bsd', weighted, o_w.reshape(H, E, P, D))
        return out
    x = L0_attn_x
    xn = _layernorm(x, axis=-1)
    x = x + _L0_attn_ref(xn, L0_attn_Wq, L0_attn_bq, L0_attn_Wk, L0_attn_bk, L0_attn_Wv, L0_attn_bv, L0_attn_Wo, L0_attn_bo) + _L0_ffn_ref(xn, L0_ffn_q_w, L0_ffn_k_w, L0_ffn_v_w, L0_ffn_o_w, L0_ffn_sel_v_w, L0_ffn_sel_o_w, L0_ffn_route_scale)
    return x

_drawn_inputs = setup_inputs


def setup_inputs(seed=0):
    import zlib

    import numpy as np

    out = dict(_drawn_inputs(seed))
    spreads = {'L0_attn_bq': (0.0, 0.1),
     'L0_attn_bk': (0.0, 0.1),
     'L0_attn_bv': (0.0, 0.1),
     'L0_attn_bo': (0.0, 0.8)}
    factors = {'L0_ffn_q_w': 8.0,
     'L0_ffn_k_w': 8.0,
     'L0_ffn_v_w': 8.0,
     'L0_ffn_o_w': 8.0,
     'L0_ffn_sel_v_w': 8.0,
     'L0_ffn_sel_o_w': 8.0}
    for name, (base, spread) in spreads.items():
        noise = np.random.default_rng([zlib.crc32(name.encode()), seed]).standard_normal(out[name].shape)
        drawn = base * np.exp(spread * noise) if base else spread * noise
        out[name] = jnp.asarray(drawn.astype(out[name].dtype))
    for name, factor in factors.items():
        out[name] = (out[name] * factor).astype(out[name].dtype)
    return out
```

```python
from contextlib import ExitStack

import concourse.bass as bass
from concourse import mybir

ALU = mybir.AluOpType
ACT = mybir.ActivationFunctionType
F32 = mybir.dt.float32
F32R = mybir.dt.float32r
AX_X = mybir.AxisListType.X

P = 128
LN_EPS = 1e-5
NORM_EPS = 1e-6
TINY = 1e-30
CHUNK = 32
FIRST = 1


def block_kernel(nc, x, Wq, bq, Wk, bk, Wv, bv, Wo, bo, q_w, k_w, v_w, o_w, sel_v_w, sel_o_w, route_scale, out):
    NB, SEQ, D = x.shape
    NH = q_w.shape[0] // P
    NE = v_w.shape[0] // NH
    TB = SEQ // P
    NT = NB * TB
    NCH = SEQ // CHUNK
    GH = NE // 2
    GATES = 2 * NH * NE
    SCALE = float(P) ** -0.5
    assert D == P and NB * CHUNK == P and GATES == P and GH * P == 512 and SEQ == 512

    with ExitStack() as ctx:
        def sb(name, shape, dt=F32):
            return ctx.enter_context(nc.sbuf_tensor(name, shape, dt))

        def bank(name):
            return ctx.enter_context(nc.psum_tensor(name, [P, 512], F32))

        def sem(name):
            return ctx.enter_context(nc.semaphore(name))

        x_sb = sb("x_sb", [P, NT, D])
        xn = sb("xn", [P, NT, D])
        xh = sb("xh", [P, NT * P], F32R)
        xl = sb("xl", [P, NT * P], F32R)
        stats = sb("stats", [P, NT, 6])
        mv = sb("mv", [P, NT, 2])
        rstd = sb("rstd", [P, NT])
        small_a = sb("small_a", [P, NT])
        small_b = sb("small_b", [P, NT])
        ident = sb("ident", [P, P])
        w4 = sb("w4", [P, 4, D])
        w3h = sb("w3h", [P, 3 * P], F32R)
        w3l = sb("w3l", [P, 3 * P], F32R)
        woT = sb("woT", [P, P])
        sel = sb("sel", [P, D])
        selh = sb("selh", [P, P], F32R)
        sell = sb("sell", [P, P], F32R)
        bias3 = sb("bias3", [P, 3, P])
        bo_b = sb("bo_b", [P, P])
        rs_b = sb("rs_b", [P, 1])
        qkv = sb("qkv", [P, NT, 3, P])
        kq = sb("kq", [P, NT])
        kk = sb("kk", [P, NT])
        kn = sb("kn", [P, NT])
        scrap_v = sb("scrap_v", [P, P])
        scrap_a = sb("scrap_a", [P, P])
        uT = sb("uT", [P, NB, SEQ])
        qT = sb("qT", [P, NB, SEQ])
        prob = sb("prob", [P, NT, GATES])
        pick = sb("pick", [P, NT, GATES])
        tmpg = sb("tmpg", [P, NT, GATES])
        gate = sb("gate", [P, NT, GATES])
        rank = sb("rank", [P, NE])
        NG = NT * 2 * NH
        top1 = sb("top1", [P, NG])
        top2 = sb("top2", [P, NG])
        topr = sb("topr", [P, NG])
        A = sb("A", [P, NB, P])
        uTc = sb("uTc", [P, NB, CHUNK])
        AuT = sb("AuT", [P, NB, CHUNK])
        uA = sb("uA", [P, P])
        M = sb("M", [P, 2 * CHUNK])
        eye32 = sb("eye32", [P, CHUNK])
        nmask = sb("nmask", [P, CHUNK])
        nlow = sb("nlow", [P, P])
        row = sb("row", [P, CHUNK + 1])
        rp = sb("rp", [P, 1])
        cf = sb("cf", [P, 1])
        Dv = sb("Dv", [P, 1])
        rD = sb("rD", [P, 1])
        rDf = sb("rDf", [P, 1])
        scr32 = sb("scr32", [P, CHUNK])
        Rbd = sb("Rbd", [P, P])
        Wc = sb("Wc", [P, P])
        Zc = sb("Zc", [P, P])
        Zbd = sb("Zbd", [P, NB, P])
        zT = sb("zT", [P, NB, SEQ])
        causal = sb("causal", [P, P])
        pT = sb("pT", [P, 2, 512])
        oT = sb("oT", [P, 512])
        qk_raw = sb("qk_raw", [P, 2, P])
        Ah = sb("Ah", [P, P], F32R)
        Al = sb("Al", [P, P], F32R)
        vo_raw = sb("vo_raw", [P, 2, NE * P])
        vo_h = sb("vo_h", [P, 2, NE * P], F32R)
        vo_l = sb("vo_l", [P, 2, NE * P], F32R)
        Th = sb("Th", [P, 512], F32R)
        Tl = sb("Tl", [P, 512], F32R)
        gh = sb("gh", [P, 2, NT, NE])
        goh = sb("goh", [P, 2, TB, NE])
        nmax = sb("nmax", [P, 2, TB])
        rsum = sb("rsum", [P, 2, TB])
        rinv = sb("rinv", [P, TB])
        prb = sb("prb", [P, TB, 512])
        pTh = sb("pTh", [P, 2, 512], F32R)
        pTl = sb("pTl", [P, 2, 512], F32R)
        Va = sb("Va", [P, TB, P])
        Vb = sb("Vb", [P, TB, P])
        Vh = sb("Vh", [P, 512], F32R)
        Vl = sb("Vl", [P, 512], F32R)
        ch = sb("ch", [P, 512], F32R)
        cl = sb("cl", [P, 512], F32R)
        tmp = sb("tmp", [P, 2, GH, P])
        half = sb("half", [P, 2, P])
        quart = sb("quart", [P, P])
        acc, acc2 = prob, pick

        bS = [bank("bS0"), bank("bS1")]
        bPT = bank("bPT")
        bC = bank("bC")
        bY = [bank("bY0"), bank("bY1")]
        bG = bank("bG")
        bU = bank("bU")

        def sems(names):
            return [sem(n) for n in names.split()]

        ld_x, ld_w, ld_b, ld_qk, ld_vo, stored, zero_ok, ident_ok, pro_p = sems(
            "ld_x ld_w ld_b ld_qk ld_vo stored zero_ok ident_ok pro_p")
        var_ok, root_ok, xn_ok, kk_ok, kroot_ok, unit_ok, link_ok, gate_ok, acc_ok = sems(
            "var_ok root_ok xn_ok kk_ok kroot_ok unit_ok link_ok gate_ok acc_ok")
        xT_mm, xh_ok, xl_ok, wT_mm, wh_ok, wl_ok, qkv_mm, qkv_ok, lg_mm = sems(
            "xT_mm xh_ok xl_ok wT_mm wh_ok wl_ok qkv_mm qkv_ok lg_mm")
        lg_ok, ut_mm, ut_ok, c_uT, c_au, c_auE, c_g, c_fac, elim_ok = sems(
            "lg_ok ut_mm ut_ok c_uT c_au c_auE c_g c_fac elim_ok")
        c_W, c_WE, c_z, c_zE, c_up, c_A, s_A, s_T, s_S = sems(
            "c_W c_WE c_z c_zE c_up c_A s_A s_T s_S")
        s_Y0, s_Y1, s_PT, s_PV, a_A, d_A, a_wh, p_wl, a_T = sems(
            "s_Y0 s_Y1 s_PT s_PV a_A d_A a_wh p_wl a_T")
        d_T, d_max, a_exp, d_gate, d_gh, d_V, a_Vh, d_Vl, a_cp = sems(
            "d_T d_max a_exp d_gate d_gh d_V a_Vh d_Vl a_cp")
        p_half, p_quart, p_acc, a_PTh, d_PTl, a_C, d_C, d_rinv, d_goh = sems(
            "p_half p_quart p_acc a_PTh d_PTl a_C d_C d_rinv d_goh")
        f_p, f_diag, f_rest, f_o, f_oE, f_y, f_take, f_res = sems(
            "f_p f_diag f_rest f_o f_oE f_y f_take f_res")
        block = ctx.enter_context(nc.Block())

        x_v = x.rearrange("b (k p) d -> p (b k) d", p=P)
        out_v = out.rearrange("b (k p) d -> p (b k) d", p=P)
        qw_v = q_w.rearrange("(h p) d -> p h d", p=P)
        kw_v = k_w.rearrange("(h p) d -> p h d", p=P)
        vw_v = v_w.rearrange("(h e) d p -> d h e p", e=NE)
        ow_v = o_w.rearrange("(h e) p d -> p h e d", e=NE)

        def v_at(b, i):
            return i if b == 0 else 2 * TB * b - TB + i

        def o_at(b, j):
            return (2 * TB * (b + 1) if b < NB - 1 else 2 * TB * NB - TB) + j

        GROUPS = 2 * NB * TB

        @block.sync
        def _(sp):
            for b in range(NB):
                sp.dma_start(x_sb[:, b * TB:(b + 1) * TB, :], x_v[:, b * TB:(b + 1) * TB, :]).then_inc(ld_x, 16)
            for n, w in enumerate((Wq, Wk, Wv, Wo)):
                sp.dma_start(w4[:, n, :], w).then_inc(ld_w, 16)
            sp.dma_start(sel[0:P // 2, :], sel_v_w).then_inc(ld_w, 16)
            sp.dma_start(sel[P // 2:P, :], sel_o_w).then_inc(ld_w, 16)
            for n, w in enumerate((bq, bk, bv)):
                sp.dma_start(bias3[:, n, :], w.rearrange("(a d) -> a d", a=1).broadcast_to([P, P])).then_inc(ld_b, 16)
            sp.dma_start(bo_b[:], bo.rearrange("(a d) -> a d", a=1).broadcast_to([P, P])).then_inc(ld_b, 16)
            sp.dma_start(rs_b[:], route_scale.rearrange("(a d) -> a d", a=1).broadcast_to([P, 1])).then_inc(ld_b, 16)
            def load_qk(h):
                sp.dma_start(qk_raw[:, 0, :], qw_v[:, bass.ds(h, 1), :].rearrange("p a d -> p (a d)")).then_inc(ld_qk, 16)
                sp.dma_start(qk_raw[:, 1, :], kw_v[:, bass.ds(h, 1), :].rearrange("p a d -> p (a d)")).then_inc(ld_qk, 16)

            def load_vo(h):
                sp.dma_start(vo_raw[:, 0, :].rearrange("p (e d) -> p e d", e=NE),
                             vw_v[:, bass.ds(h, 1), :, :].rearrange("p a e d -> p (a e) d")).then_inc(ld_vo, 16)
                sp.dma_start(vo_raw[:, 1, :].rearrange("p (e d) -> p e d", e=NE),
                             ow_v[:, bass.ds(h, 1), :, :].rearrange("p a e d -> p (a e) d")).then_inc(ld_vo, 16)

            load_qk(0)
            load_vo(0)
            with sp.Fori(1, NH) as h:
                sp.wait_ge(s_A, h)
                load_qk(h)
                sp.wait_ge(a_wh, h * 2)
                sp.wait_ge(p_wl, h * 2)
                load_vo(h)
            for b in range(NB):
                sp.wait_ge(f_res, b + 1)
                sp.dma_start(out_v[:, b * TB:(b + 1) * TB, :], x_sb[:, b * TB:(b + 1) * TB, :]).then_inc(stored, 16)
            sp.wait_ge(stored, 16 * NB)

        @block.gpsimd
        def _(pool):
            for started in (p_quart, p_acc, p_half):
                pool.sem_inc(started, FIRST)
            g = nc.gpsimd
            g.memset(ident[:], 0.0).then_inc(pro_p, 1)
            g.memset(nlow[:], -1.0).then_inc(pro_p, 1)
            g.memset(causal[:], 1.0).then_inc(pro_p, 1)
            pool.wait_ge(pro_p, 3)
            g.affine_select(out=ident[:], in_=ident[:], compare_op=ALU.not_equal, fill=1.0, base=0,
                            pattern=[[-1, P]], channel_multiplier=1).then_inc(ident_ok, 1)
            g.affine_select(out=nlow[:], in_=nlow[:], compare_op=ALU.is_gt, fill=0.0, base=0,
                            pattern=[[-1, P]], channel_multiplier=1).then_inc(ident_ok, 1)
            g.affine_select(out=causal[:], in_=causal[:], compare_op=ALU.is_ge, fill=0.0, base=0,
                            pattern=[[1, P]], channel_multiplier=-1).then_inc(ident_ok, 1)
            for e in range(NE):
                g.memset(rank[:, e:e + 1], float(NE - e)).then_inc(zero_ok, 1)
            g.memset(Rbd[:], 0.0).then_inc(zero_ok, 1)
            g.memset(Zbd[:], 0.0).then_inc(zero_ok, 1)
            pool.wait_ge(gate_ok, 1)
            g.memset(acc[:], 0.0).then_inc(acc_ok, 1)
            g.memset(acc2[:], 0.0).then_inc(acc_ok, 1)
            pool.wait_ge(acc_ok, 2)

            with pool.Fori(0, NH) as h:
                for n in range(2):
                    pool.wait_ge(a_wh, h * 2 + n + 1)
                    g.tensor_tensor(vo_l[:, n, :], vo_raw[:, n, :], vo_h[:, n, :].bitcast(F32), ALU.subtract).then_inc(p_wl, 1)

                def fold(n):
                    pool.wait_ge(p_quart, FIRST + h * GROUPS + n)
                    pool.wait_ge(a_cp, FIRST + h * (GH * GROUPS) + GH * (n + 1))
                    g.tensor_tensor(half[:], tmp[:, n % 2, 0:2, :], tmp[:, n % 2, 2:4, :], ALU.add).then_inc(p_half, 1)
                    pool.wait_ge(p_half, FIRST + h * GROUPS + n + 1)

                def value(b, i):
                    fold(v_at(b, i))
                    g.tensor_tensor(Vb[:, i, :], half[:, 0, :], half[:, 1, :], ALU.add).then_inc(p_quart, 1)

                def output(b, j):
                    n = o_at(b, j)
                    fold(n)
                    pool.wait_ge(p_acc, FIRST + h * (NB * TB) + b * TB + j)
                    g.tensor_tensor(quart[:], half[:, 0, :], half[:, 1, :], ALU.add).then_inc(p_quart, 1)
                    pool.wait_ge(p_quart, FIRST + h * GROUPS + n + 1)
                    k = b * TB + j
                    g.tensor_tensor(acc2[:, k, :], acc2[:, k, :], quart[:], ALU.add).then_inc(p_acc, 1)

                for b in range(NB):
                    pool.wait_ge(d_V, FIRST + h * NB + b)
                    for i in range(TB):
                        value(b, i)
                    for j in range(TB):
                        if b:
                            output(b - 1, j)
                for j in range(TB):
                    output(NB - 1, j)

        @block.tensor
        def _(pe):
            for started in (c_g, s_Y1, s_PV):
                pe.sem_inc(started, FIRST)
            t = nc.tensor

            def mm3(out_, ah, al, bh, bl, start=True, stop=True):
                t.matmul(out_, ah, bh, start=start, stop=False)
                t.matmul(out_, ah, bl, start=False, stop=False)
                return t.matmul(out_, al, bh, start=False, stop=stop)

            pe.wait_ge(ident_ok, 1)
            pe.wait_ge(ld_w, 96)
            for n in range(4):
                t.transpose(bY[0][:, n * P:(n + 1) * P], w4[:, n, :], ident[:]).then_inc(wT_mm, 1)
            t.transpose(bY[1][:, 0:P], sel[:], ident[:]).then_inc(wT_mm, 1)
            for b in range(NB):
                pe.wait_ge(xn_ok, b + 1)
                if b >= 2:
                    pe.wait_ge(xl_ok, b - 1)
                for i in range(TB):
                    q = t.transpose(bS[b % 2][:, i * P:(i + 1) * P], xn[:, b * TB + i, :], ident[:])
                q.then_inc(xT_mm, 1)
            pe.wait_ge(wh_ok, 3)
            pe.wait_ge(wl_ok, 2)
            for k in range(NT):
                pe.wait_ge(xh_ok, k // TB + 1)
                pe.wait_ge(xl_ok, k // TB + 1)
                c = slice(k * P, (k + 1) * P)
                if k % TB == 0 and k >= 2 * TB:
                    pe.wait_ge(lg_ok, k // TB - 1)
                q = mm3(bY[k // TB % 2][:, k % TB * P:(k % TB + 1) * P], xh[:, c], xl[:, c], selh[:], sell[:])
                if k % TB == TB - 1:
                    q.then_inc(lg_mm, 1)
                if k >= 2:
                    pe.wait_ge(qkv_ok, k - 1)
                mm3((bG, bU)[k % 2][:, 0:3 * P], xh[:, c], xl[:, c], w3h[:], w3l[:]).then_inc(qkv_mm, 1)
            for n in range(2 * NB):
                b = n % NB
                pe.wait_ge(unit_ok, 1)
                if n >= 2:
                    pe.wait_ge(ut_ok, n - 1)
                for i in range(TB):
                    q = t.transpose(bS[n % 2][:, i * P:(i + 1) * P], qkv[:, b * TB + i, 1 if n < NB else 0, :], ident[:])
                q.then_inc(ut_mm, 1)

            with pe.Fori(0, NCH) as c:
                pe.wait_ge(c_uT, c + 1)
                pe.wait_ge(c_A, c + 1)
                pe.wait_ge(c_zE, FIRST + c)
                for b in range(NB):
                    t.matmul(bG[:, b * CHUNK:(b + 1) * CHUNK], A[:, b, :], uTc[:, b, :], start=True, stop=True)
                for b in range(NB):
                    q = t.matmul(bG[b * CHUNK:(b + 1) * CHUNK, P:2 * P], uTc[:, b, :], A[:, b, :], start=True, stop=True)
                q.then_inc(c_au, 1)
                pe.wait_ge(c_auE, c * 2 + 2)
                for b in range(NB):
                    q = t.matmul(bG[b * CHUNK:(b + 1) * CHUNK, 2 * P:2 * P + CHUNK], uTc[:, b, :], AuT[:, b, :], start=True, stop=True)
                q.then_inc(c_g, 1)
                pe.wait_ge(c_fac, c + 1)
                t.matmul(bG[:, 3 * P:4 * P], Rbd[:], uA[:], start=True, stop=True).then_inc(c_W, 1)
                pe.wait_ge(c_WE, c * 6 + 6)
                t.matmul(bU[:], Wc[:], Zbd[:].rearrange("p b d -> p (b d)"), start=True, stop=True).then_inc(c_up, 1)
                t.transpose(bG[:, 0:P], Zc[:], ident[:]).then_inc(c_z, 1)

            with pe.Fori(0, NH) as h:
                G0 = h * (GH * GROUPS)

                def expert(side, n, lh, ll):
                    for g, (ready, free) in enumerate(((s_Y0, d_gate), (s_Y1, a_cp))):
                        e = slice(g * 512, (g + 1) * 512)
                        pe.wait_ge(free, FIRST + G0 + GH * n)
                        mm3(bY[g][:], lh, ll, vo_h[:, side, e], vo_l[:, side, e]).then_inc(ready, 1)

                def project(b):
                    c = slice(b * 512, (b + 1) * 512)
                    mm3(bS[0][:], Ah[:], Al[:], xh[:, c], xl[:, c]).then_inc(s_T, 1)

                def output(b, j):
                    c = slice(j * P, (j + 1) * P)
                    if j == 0:
                        pe.wait_ge(a_C, h * NB + b + 1)
                        pe.wait_ge(d_C, FIRST + h * NB + b + 1)
                    expert(1, o_at(b, j), ch[:, c], cl[:, c])

                pe.wait_ge(ld_qk, h * 32 + 32)
                pe.wait_ge(d_C, FIRST + h * NB)
                t.matmul(bC[:, 0:P], qk_raw[:, 0, :], qk_raw[:, 1, :], start=True, stop=True).then_inc(s_A, 1)
                pe.wait_ge(a_A, h + 1)
                pe.wait_ge(d_A, h + 1)
                project(0)
                pe.wait_ge(a_wh, h * 2 + 2)
                pe.wait_ge(p_wl, h * 2 + 2)
                for b in range(NB):
                    pe.wait_ge(a_T, h * NB + b + 1)
                    pe.wait_ge(d_T, h * NB + b + 1)
                    for i in range(TB):
                        c = slice(i * P, (i + 1) * P)
                        kc = slice(b * 512, (b + 1) * 512)
                        if i >= 2:
                            pe.wait_ge(a_exp, h * NB * TB + b * TB + i - 1)
                        mm3(bS[i % 2][:], Th[:, c], Tl[:, c], xh[:, kc], xl[:, kc]).then_inc(s_S, 1)
                        xc = slice((b * TB + i) * P, (b * TB + i + 1) * P)
                        expert(0, v_at(b, i), xh[:, xc], xl[:, xc])
                    pe.wait_ge(a_exp, h * NB * TB + (b + 1) * TB)
                    if b < NB - 1:
                        project(b + 1)
                    for j in range(TB):
                        n = h * NB * TB + b * TB + j
                        pe.wait_ge(d_PTl, FIRST + n)
                        for i in range(TB):
                            q = t.transpose(bPT[:, i * P:(i + 1) * P], prb[:, i, j * P:(j + 1) * P], ident[:])
                        q.then_inc(s_PT, 1)
                        if b:
                            output(b - 1, j)
                        if j == 0:
                            pe.wait_ge(a_Vh, h * NB + b + 1)
                            pe.wait_ge(d_Vl, h * NB + b + 1)
                            if b:
                                pe.wait_ge(d_C, FIRST + h * NB + b)
                        pe.wait_ge(d_PTl, FIRST + n + 1)
                        vc = slice(j * P, (j + 1) * P)
                        mm3(bC[:], Vh[:, vc], Vl[:, vc], pTh[:, j % 2, :], pTl[:, j % 2, :],
                            start=(j == 0), stop=(j == TB - 1)).then_inc(s_PV, 1)
                for j in range(TB):
                    output(NB - 1, j)

            def rest(n):
                return n // TB * (TB - 1) + min(n % TB + 1, TB - 1)

            for b in range(NB):
                def weigh(i):
                    n = b * TB + i
                    pe.wait_ge(f_diag, n + 1)
                    pe.wait_ge(f_rest, rest(n))
                    if i == 0 and b:
                        pe.wait_ge(f_oE, b)
                    t.matmul(bC[:, i * P:], qkv[:, n, 2, :], pT[:, i % 2, 0:SEQ - i * P],
                             start=(i == 0), stop=(i == TB - 1)).then_inc(f_o, 1)

                for i in range(TB):
                    n = b * TB + i
                    if n >= 2:
                        pe.wait_ge(f_diag, n - 1)
                        pe.wait_ge(f_rest, rest(n - 2))
                    t.matmul(bS[i % 2][:, 0:SEQ - i * P], zT[:, b, i * P:(i + 1) * P], qT[:, b, i * P:],
                             start=True, stop=True).then_inc(f_p, 1)
                    if i:
                        weigh(i - 1)
                weigh(TB - 1)
                pe.wait_ge(f_oE, b + 1)
                pe.wait_ge(f_take, b) if b else None
                for i in range(TB):
                    q = t.matmul(bPT[:, i * P:(i + 1) * P], oT[:, i * P:(i + 1) * P], woT[:], start=True, stop=True)
                q.then_inc(f_y, 1)

        @block.scalar
        def _(act):
            for started in (a_cp, c_zE):
                act.sem_inc(started, FIRST)
            a = nc.scalar
            act.wait_ge(var_ok, 1)
            a.activation(small_a[:], rstd[:], ACT.Sqrt).then_inc(root_ok, 1)
            act.wait_ge(wT_mm, 5)
            a.activation(w3h[:], bY[0][:, 0:3 * P], ACT.Copy).then_inc(wh_ok, 1)
            a.activation(woT[:], bY[0][:, 3 * P:], ACT.Copy).then_inc(wh_ok, 1)
            a.activation(selh[:], bY[1][:, 0:P], ACT.Copy).then_inc(wh_ok, 1)
            for b in range(NB):
                act.wait_ge(xT_mm, b + 1)
                a.activation(xh[:, b * 512:(b + 1) * 512], bS[b % 2][:], ACT.Copy).then_inc(xh_ok, 1)
            for b in range(NB):
                act.wait_ge(lg_mm, b + 1)
                a.activation(prob[:, b * TB:(b + 1) * TB, :].rearrange("p a b -> p (a b)"), bY[b % 2][:], ACT.Exp, scale=-1.0).then_inc(lg_ok, 1)
            act.wait_ge(kk_ok, 1)
            a.activation(small_b[:], kk[:], ACT.Sqrt).then_inc(kroot_ok, 1)
            for n in range(2 * NB):
                act.wait_ge(ut_mm, n + 1)
                a.activation((uT if n < NB else qT)[:, n % NB, :], bS[n % 2][:], ACT.Copy).then_inc(ut_ok, 1)

            act.wait_ge(ut_ok, 2 * NB)
            with act.Fori(0, NCH) as c:
                act.wait_ge(c_g, FIRST + c)
                a.activation(uTc[:], uT[:, :, bass.ds(c * CHUNK, CHUNK)], ACT.Copy).then_inc(c_uT, 1)
                act.wait_ge(c_au, c + 1)
                a.activation(AuT[:].rearrange("p b d -> p (b d)"), bG[:, 0:P], ACT.Copy).then_inc(c_auE, 1)
                a.activation(uA[:], bG[:, P:2 * P], ACT.Copy).then_inc(c_auE, 1)
                act.wait_ge(c_W, c + 1)
                act.wait_ge(c_fac, c + 1)
                a.activation(Wc[:], bG[:, 3 * P:4 * P], ACT.Copy).then_inc(c_WE, 1)
                for b in range(NB):
                    r = slice(b * CHUNK, (b + 1) * CHUNK)
                    a.activation(Zbd[r, b, :], bG[r, 3 * P:4 * P], ACT.Copy, scale=rDf[r, :]).then_inc(c_WE, 1)
                a.activation(Zc[:], bG[:, 3 * P:4 * P], ACT.Copy, scale=rDf[:]).then_inc(c_WE, 1)
                act.wait_ge(c_z, c + 1)
                a.activation(zT[:, :, bass.ds(c * CHUNK, CHUNK)], bG[:, 0:P].rearrange("p (b d) -> p b d", b=NB), ACT.Copy).then_inc(c_zE, 1)

            with act.Fori(0, NH) as h:
                def scaled(n, g4, k):
                    act.wait_ge(s_Y1, FIRST + h * GROUPS + n + 1)
                    if n >= 2:
                        act.wait_ge(p_half, FIRST + h * GROUPS + n - 1)
                    else:
                        act.wait_ge(p_half, FIRST + h * GROUPS)
                    for e in range(GH):
                        a.activation(tmp[:, n % 2, e, :], bY[1][:, e * P:(e + 1) * P], ACT.Copy,
                                     scale=g4[:, k, GH + e:GH + e + 1]).then_inc(a_cp, 1)

                def project(b):
                    act.wait_ge(s_T, h * NB + b + 1)
                    a.activation(Th[:], bS[0][:], ACT.Copy).then_inc(a_T, 1)

                act.wait_ge(s_A, h + 1)
                a.activation(Ah[:], bC[:, 0:P], ACT.Copy, scale=SCALE).then_inc(a_A, 1)
                act.wait_ge(ld_vo, h * 32 + 32)
                for n in range(2):
                    act.wait_ge(s_Y1, FIRST + h * GROUPS)
                    a.activation(vo_h[:, n, :], vo_raw[:, n, :], ACT.Copy).then_inc(a_wh, 1)
                project(0)
                act.wait_ge(d_gh, h * 2 + 2)
                for b in range(NB):
                    for i in range(TB):
                        n = h * NB * TB + b * TB + i
                        act.wait_ge(d_max, n + 1)
                        a.activation(prb[:, i, :], bS[i % 2][:], ACT.Exp, bias=nmax[:, b % 2, i:i + 1],
                                     accum_out=rsum[:, b % 2, i:i + 1]).then_inc(a_exp, 1)
                        scaled(v_at(b, i), gh[:, 0, :, :], b * TB + i)
                    if b < NB - 1:
                        project(b + 1)
                    for j in range(TB):
                        n = h * NB * TB + b * TB + j
                        act.wait_ge(s_PT, n + 1)
                        if j == 0:
                            act.wait_ge(s_PV, FIRST + h * NB * TB + b * TB)
                        if j >= 2:
                            act.wait_ge(s_PV, FIRST + n - 1)
                        a.activation(pTh[:, j % 2, :], bPT[:], ACT.Copy).then_inc(a_PTh, 1)
                        if j == 0:
                            act.wait_ge(d_V, FIRST + h * NB + b + 1)
                            a.activation(Vh[:], Va[:].rearrange("p b d -> p (b d)"), ACT.Copy).then_inc(a_Vh, 1)
                        if b:
                            if j == 0:
                                act.wait_ge(d_goh, h * NB + b)
                            scaled(o_at(b - 1, j), goh[:, (b - 1) % 2, :, :], j)
                    act.wait_ge(s_PV, FIRST + h * NB * TB + (b + 1) * TB)
                    a.activation(ch[:], bC[:], ACT.Copy).then_inc(a_C, 1)
                act.wait_ge(d_goh, h * NB + NB)
                for j in range(TB):
                    scaled(o_at(NB - 1, j), goh[:, (NB - 1) % 2, :, :], j)

            for b in range(NB):
                for i in range(TB - 1):
                    act.wait_ge(f_diag, b * TB + i + 1)
                    w = SEQ - i * P
                    a.activation(pT[:, i % 2, P:w], bS[i % 2][:, P:w], ACT.Copy).then_inc(f_rest, 1)
                act.wait_ge(f_o, (b + 1) * TB)
                a.activation(oT[:], bC[:], ACT.Copy).then_inc(f_oE, 1)

        @block.vector
        def _(dve):
            for started in (d_V, d_gate, d_C, d_PTl):
                dve.sem_inc(started, FIRST)
            v = nc.vector
            linked = [0]

            def link(ins):
                linked[0] += 1
                ins.then_inc(link_ok, 1)
                dve.wait_ge(link_ok, linked[0])

            def wide(g2):
                return g2[:].rearrange("p (g a) -> p g a", a=1).broadcast_to([P, NG, NE])

            def grouped(g3):
                return g3[:].rearrange("p k (g e) -> p (k g) e", e=NE)

            dve.wait_ge(ld_x, 16 * NB)
            for k in range(NT):
                q = v.bn_stats(stats[:, k, :], x_sb[:, k, :])
            link(q)
            for k in range(NT):
                q = v.bn_aggr(mv[:, k, :], stats[:, k, :])
            link(q)
            v.tensor_scalar(rstd[:], mv[:, :, 1], LN_EPS, None, ALU.add).then_inc(var_ok, 1)
            dve.wait_ge(root_ok, 1)
            dve.wait_ge(var_ok, 1)
            link(v.reciprocal(small_b[:], small_a[:]))
            link(v.tensor_tensor(small_a[:], small_b[:], small_b[:], ALU.mult))
            link(v.tensor_tensor(small_a[:], small_a[:], rstd[:], ALU.mult))
            link(v.tensor_scalar(small_a[:], small_a[:], -0.5, 1.5, ALU.mult, ALU.add))
            link(v.tensor_tensor(rstd[:], small_a[:], small_b[:], ALU.mult))
            for k in range(NT):
                q = v.tensor_scalar(xn[:, k, :], x_sb[:, k, :], mv[:, k, 0:1], rstd[:, k:k + 1], ALU.subtract, ALU.mult)
                if k % TB == TB - 1:
                    q.then_inc(xn_ok, 1)
            dve.wait_ge(wh_ok, 3)
            v.tensor_tensor(w3l[:], bY[0][:, 0:3 * P], w3h[:].bitcast(F32), ALU.subtract).then_inc(wl_ok, 1)
            v.tensor_tensor(sell[:], bY[1][:, 0:P], selh[:].bitcast(F32), ALU.subtract).then_inc(wl_ok, 1)
            for b in range(NB):
                dve.wait_ge(xh_ok, b + 1)
                c = slice(b * 512, (b + 1) * 512)
                v.tensor_tensor(xl[:, c], bS[b % 2][:], xh[:, c].bitcast(F32), ALU.subtract).then_inc(xl_ok, 1)
            dve.wait_ge(ld_b, 80)
            for k in range(NT):
                dve.wait_ge(qkv_mm, k + 1)
                v.tensor_tensor(qkv[:, k, :, :], (bG, bU)[k % 2][:, 0:3 * P].rearrange("p (a b) -> p a b", a=3),
                                bias3[:], ALU.add).then_inc(qkv_ok, 1)
            dve.wait_ge(qkv_ok, NT)
            for k in range(NT):
                link(v.tensor_tensor_reduce(scrap_v[:], qkv[:, k, 0, :], qkv[:, k, 1, :], 1.0, 0.0, ALU.mult, ALU.add, kq[:, k:k + 1]))
            for k in range(NT):
                link(v.tensor_tensor_reduce(scrap_v[:], qkv[:, k, 1, :], qkv[:, k, 1, :], 1.0, 0.0, ALU.mult, ALU.add, kk[:, k:k + 1]))
            v.tensor_scalar(kk[:], kk[:], 1.0, None, ALU.mult).then_inc(kk_ok, 1)
            dve.wait_ge(kk_ok, 1)
            dve.wait_ge(kroot_ok, 1)
            link(v.tensor_scalar(small_a[:], small_b[:], TINY, None, ALU.max))
            link(v.reciprocal(small_a[:], small_a[:]))
            link(v.tensor_tensor(small_a[:], small_a[:], kk[:], ALU.mult))
            link(v.tensor_tensor(small_a[:], small_a[:], small_b[:], ALU.add))
            link(v.tensor_scalar(small_a[:], small_a[:], 0.5, NORM_EPS, ALU.mult, ALU.add))
            link(v.reciprocal(kn[:], small_a[:]))
            for k in range(NT):
                v.tensor_scalar(qkv[:, k, 1, :], qkv[:, k, 1, :], kn[:, k:k + 1], None, ALU.mult)
                q = v.tensor_scalar(qkv[:, k, 2, :], qkv[:, k, 2, :], kq[:, k:k + 1], None, ALU.mult)
            q.then_inc(unit_ok, 1)
            dve.wait_ge(lg_ok, NB)
            dve.wait_ge(zero_ok, NE + 2)
            link(v.tensor_scalar(prob[:], prob[:], 1.0, None, ALU.add))
            link(v.reciprocal(prob[:], prob[:]))
            ranks = rank[:].rearrange("p (a e) -> p a e", a=1).broadcast_to([P, NG, NE])
            link(v.tensor_reduce(top1[:], grouped(prob), AX_X, ALU.max))
            link(v.tensor_tensor(grouped(pick), grouped(prob), wide(top1), ALU.is_equal))
            link(v.tensor_tensor(grouped(pick), grouped(pick), ranks, ALU.mult))
            link(v.tensor_reduce(topr[:], grouped(pick), AX_X, ALU.max))
            link(v.tensor_tensor(grouped(pick), grouped(pick), wide(topr), ALU.is_equal))
            link(v.scalar_tensor_tensor(out=tmpg[:], in0=pick[:], scalar=-2.0, in1=prob[:], op0=ALU.mult, op1=ALU.add))
            link(v.tensor_reduce(top2[:], grouped(tmpg), AX_X, ALU.max))
            link(v.tensor_tensor(grouped(tmpg), grouped(tmpg), wide(top2), ALU.is_equal))
            link(v.tensor_tensor(grouped(tmpg), grouped(tmpg), ranks, ALU.mult))
            link(v.tensor_reduce(topr[:], grouped(tmpg), AX_X, ALU.max))
            link(v.tensor_tensor(grouped(tmpg), grouped(tmpg), wide(topr), ALU.is_equal))
            link(v.tensor_tensor(pick[:], pick[:], tmpg[:], ALU.add))
            link(v.tensor_tensor(gate[:], pick[:], prob[:], ALU.mult))
            link(v.tensor_tensor(topr[:], top1[:], top2[:], ALU.add))
            link(v.tensor_scalar(topr[:], topr[:], 1e-9, None, ALU.max))
            link(v.reciprocal(topr[:], topr[:]))
            link(v.tensor_scalar(topr[:], topr[:], rs_b[:, 0:1], None, ALU.mult))
            link(v.tensor_tensor(grouped(gate), grouped(gate), wide(topr), ALU.mult))
            v.tensor_scalar(rs_b[:], rs_b[:], 1.0, None, ALU.mult).then_inc(gate_ok, 1)
            dve.wait_ge(ident_ok, 3)
            for b in range(NB):
                r = slice(b * CHUNK, (b + 1) * CHUNK)
                link(v.tensor_copy(eye32[r, :], ident[r, r]))
                link(v.tensor_copy(nmask[r, :], nlow[r, r]))
            for b in range(NB):
                q = v.tensor_copy(A[:, b, :], ident[:])
            q.then_inc(c_A, 1)
            with dve.Fori(0, NCH) as c:
                n = [0]
                dve.sem_clear(elim_ok)

                def step(ins):
                    n[0] += 1
                    ins.then_inc(elim_ok, 1)
                    dve.wait_ge(elim_ok, n[0])

                dve.wait_ge(c_g, FIRST + c + 1)
                step(v.tensor_tensor(M[:, 0:CHUNK], bG[:, 2 * P:2 * P + CHUNK], eye32[:], ALU.add))
                step(v.tensor_copy(M[:, CHUNK:], eye32[:]))
                for k in range(CHUNK - 1):
                    step(v.stream_shuffle(row[:], M[:, k:k + CHUNK + 1], [k] * CHUNK))
                    step(v.reciprocal(rp[:], row[:, 0:1]))
                    step(v.scalar_tensor_tensor(out=cf[:], in0=M[:, k:k + 1], scalar=rp[:, 0:1], in1=nmask[:, k:k + 1],
                                                op0=ALU.mult, op1=ALU.mult))
                    step(v.scalar_tensor_tensor(out=M[:, k + 1:k + CHUNK + 1], in0=row[:, 1:], scalar=cf[:, 0:1],
                                                in1=M[:, k + 1:k + CHUNK + 1], op0=ALU.mult, op1=ALU.add))
                step(v.tensor_tensor_reduce(scr32[:], M[:, 0:CHUNK], eye32[:], 1.0, 0.0, ALU.mult, ALU.add, Dv[:]))
                step(v.reciprocal(rD[:], Dv[:]))
                for b in range(NB):
                    r = slice(b * CHUNK, (b + 1) * CHUNK)
                    step(v.transpose(Rbd[r, r], M[r, CHUNK:]))
                v.tensor_copy(rDf[:], rD[:]).then_inc(c_fac, 1)
                dve.wait_ge(c_up, c + 1)
                v.tensor_tensor(A[:].rearrange("p b d -> p (b d)"), A[:].rearrange("p b d -> p (b d)"), bU[:],
                                ALU.subtract).then_inc(c_A, 1)

            with dve.Fori(0, NH) as h:
                G0 = h * (GH * GROUPS)

                def gated(n, into, g4, k, fresh):
                    dve.wait_ge(s_Y0, h * GROUPS + n + 1)
                    for e in range(GH):
                        dve.wait_ge(d_gate, FIRST + G0 + GH * n + e)
                        y, g1 = bY[0][:, e * P:(e + 1) * P], g4[:, k, e:e + 1]
                        if fresh and e == 0:
                            q = v.tensor_scalar(into, y, g1, None, ALU.mult)
                        else:
                            q = v.scalar_tensor_tensor(out=into, in0=y, scalar=g1, in1=into, op0=ALU.mult, op1=ALU.add)
                        q.then_inc(d_gate, 1)

                def project(b):
                    dve.wait_ge(a_T, h * NB + b + 1)
                    v.tensor_tensor(Tl[:], bS[0][:], Th[:].bitcast(F32), ALU.subtract).then_inc(d_T, 1)

                def output(b, j):
                    if j == 0:
                        dve.wait_ge(d_goh, h * NB + b + 1)
                    gated(o_at(b, j), acc[:, b * TB + j, :], goh[:, b % 2, :, :], j, False)

                dve.wait_ge(acc_ok, 2)
                dve.wait_ge(a_A, h + 1)
                v.scalar_tensor_tensor(out=Al[:], in0=bC[:, 0:P], scalar=SCALE, in1=Ah[:].bitcast(F32),
                                       op0=ALU.mult, op1=ALU.subtract).then_inc(d_A, 1)
                dve.wait_ge(a_cp, FIRST + G0)
                dve.wait_ge(d_gate, FIRST + G0)
                v.tensor_copy(gh[:, 0, :, :], gate[:, :, bass.ds(h * NE, NE)]).then_inc(d_gh, 1)
                v.tensor_copy(gh[:, 1, :, :], gate[:, :, bass.ds(NH * NE + h * NE, NE)]).then_inc(d_gh, 1)
                project(0)
                dve.wait_ge(d_gh, h * 2 + 2)
                for b in range(NB):
                    for i in range(TB):
                        n = h * NB * TB + b * TB + i
                        dve.wait_ge(s_S, n + 1)
                        v.tensor_reduce(nmax[:, b % 2, i:i + 1], bS[i % 2][:], AX_X, ALU.max, negate=True).then_inc(d_max, 1)
                        gated(v_at(b, i), Va[:, i, :], gh[:, 0, :, :], b * TB + i, True)
                    if b < NB - 1:
                        project(b + 1)
                    dve.wait_ge(p_quart, FIRST + h * GROUPS + v_at(b, TB - 1) + 1)
                    dve.wait_ge(d_gate, FIRST + G0 + GH * (v_at(b, TB - 1) + 1))
                    v.tensor_tensor(Va[:], Va[:], Vb[:], ALU.add).then_inc(d_V, 1)
                    dve.wait_ge(a_exp, h * NB * TB + (b + 1) * TB)
                    v.reciprocal(rinv[:], rsum[:, b % 2, :]).then_inc(d_rinv, 1)
                    dve.wait_ge(d_rinv, h * NB + b + 1)
                    if b >= 2:
                        dve.wait_ge(a_cp, FIRST + G0 + GH * (o_at(b - 2, TB - 1) + 1))
                    v.tensor_tensor(goh[:, b % 2, :, :], gh[:, 1, b * TB:(b + 1) * TB, :],
                                    rinv[:].rearrange("p (k a) -> p k a", a=1).broadcast_to([P, TB, NE]), ALU.mult).then_inc(d_goh, 1)
                    for j in range(TB):
                        n = h * NB * TB + b * TB + j
                        dve.wait_ge(a_PTh, n + 1)
                        v.tensor_tensor(pTl[:, j % 2, :], bPT[:], pTh[:, j % 2, :].bitcast(F32), ALU.subtract).then_inc(d_PTl, 1)
                        if j == 0:
                            dve.wait_ge(a_Vh, h * NB + b + 1)
                            v.tensor_tensor(Vl[:], Va[:].rearrange("p b d -> p (b d)"), Vh[:].bitcast(F32), ALU.subtract).then_inc(d_Vl, 1)
                        if b:
                            output(b - 1, j)
                    dve.wait_ge(a_C, h * NB + b + 1)
                    v.tensor_tensor(cl[:], bC[:], ch[:].bitcast(F32), ALU.subtract).then_inc(d_C, 1)
                for j in range(TB):
                    output(NB - 1, j)

            dve.wait_ge(p_acc, FIRST + NH * NB * TB)
            dve.wait_ge(d_gate, FIRST + NH * GH * GROUPS)
            for b in range(NB):
                for i in range(TB):
                    dve.wait_ge(f_p, b * TB + i + 1)
                    v.tensor_tensor(pT[:, i % 2, 0:P], bS[i % 2][:, 0:P], causal[:], ALU.mult).then_inc(f_diag, 1)
                k = slice(b * TB, (b + 1) * TB)
                link(v.tensor_tensor(xn[:, k, :], acc[:, k, :], acc2[:, k, :], ALU.add))
                link(v.tensor_tensor(xn[:, k, :], xn[:, k, :], x_sb[:, k, :], ALU.add))
                link(v.tensor_tensor(xn[:, k, :], xn[:, k, :], bo_b[:].rearrange("p (a d) -> p a d", a=1).broadcast_to([P, TB, P]), ALU.add))
                dve.wait_ge(f_y, b + 1)
                q = v.tensor_tensor(xn[:, k, :].rearrange("p k d -> p (k d)"), xn[:, k, :].rearrange("p k d -> p (k d)"), bPT[:], ALU.add)
                q.then_inc(f_take, 1)
                dve.wait_ge(f_take, b + 1)
                q = v.tensor_scalar(x_sb[:, k, :], xn[:, k, :], 1.0, None, ALU.mult)
                q.then_inc(f_res, 1)


_INS = ['L0_attn_x', 'L0_attn_Wq', 'L0_attn_bq', 'L0_attn_Wk', 'L0_attn_bk', 'L0_attn_Wv', 'L0_attn_bv', 'L0_attn_Wo', 'L0_attn_bo',
        'L0_ffn_q_w', 'L0_ffn_k_w', 'L0_ffn_v_w', 'L0_ffn_o_w', 'L0_ffn_sel_v_w', 'L0_ffn_sel_o_w', 'L0_ffn_route_scale']


def kernel(**inputs):
    import numpy as np
    import concourse.bacc as bacc
    from concourse.bass_utils import run_bass_kernel_spmd

    nc = bacc.Bacc("TRN2", target_bir_lowering=False, num_devices=1)
    arrays, args = {}, []
    for name in _INS:
        a = np.ascontiguousarray(inputs[name])
        arrays[name] = a
        args.append(nc.dram_tensor(name, a.shape, mybir.dt.from_np(a.dtype), kind="ExternalInput").ap())
    shape = inputs['L0_attn_x'].shape
    out = nc.dram_tensor("out", shape, F32, kind="ExternalOutput").ap()
    block_kernel(nc, *args, out)
    r = run_bass_kernel_spmd(nc, [arrays], core_ids=[0])
    return r.results[0]["out"]
```

```python
from contextlib import ExitStack

import concourse.bass as bass
from concourse import mybir

ALU = mybir.AluOpType
ACT = mybir.ActivationFunctionType
F32 = mybir.dt.float32
F32R = mybir.dt.float32r
AX_X = mybir.AxisListType.X

P = 128
LN_EPS = 1e-5
NORM_EPS = 1e-6
TINY = 1e-30
CHUNK = 32
FIRST = 8


def block_kernel(nc, x, Wq, bq, Wk, bk, Wv, bv, Wo, bo, q_w, k_w, v_w, o_w, sel_v_w, sel_o_w, route_scale, out):
    NB, SEQ, D = x.shape
    NH = q_w.shape[0] // P
    NE = v_w.shape[0] // NH
    TB = SEQ // P
    NT = NB * TB
    NCH = SEQ // CHUNK
    GH = NE // 2
    GATES = 2 * NH * NE
    SCALE = float(P) ** -0.5
    assert D == P and NB * CHUNK == P and GATES == P and GH * P == 512 and SEQ == 512

    with ExitStack() as ctx:
        def sb(name, shape, dt=F32):
            return ctx.enter_context(nc.sbuf_tensor(name, shape, dt))

        def bank(name):
            return ctx.enter_context(nc.psum_tensor(name, [P, 512], F32))

        def sem(name):
            return ctx.enter_context(nc.semaphore(name))

        x_sb = sb("x_sb", [P, NT, D])
        xn = sb("xn", [P, NT, D])
        xh = sb("xh", [P, NT * P], F32R)
        xl = sb("xl", [P, NT * P], F32R)
        stats = sb("stats", [P, NT, 6])
        mv = sb("mv", [P, NT, 2])
        rstd = sb("rstd", [P, NT])
        small_a = sb("small_a", [P, NT])
        small_b = sb("small_b", [P, NT])
        ident = sb("ident", [P, P])
        w4 = sb("w4", [P, 4, D])
        w3h = sb("w3h", [P, 3 * P], F32R)
        w3l = sb("w3l", [P, 3 * P], F32R)
        woT = sb("woT", [P, P])
        sel = sb("sel", [P, D])
        selh = sb("selh", [P, P], F32R)
        sell = sb("sell", [P, P], F32R)
        bias3 = sb("bias3", [P, 3, P])
        bo_b = sb("bo_b", [P, P])
        rs_b = sb("rs_b", [P, 1])
        qkv = sb("qkv", [P, NT, 3, P])
        kq = sb("kq", [P, NT])
        kk = sb("kk", [P, NT])
        kn = sb("kn", [P, NT])
        scrap_v = sb("scrap_v", [P, P])
        scrap_a = sb("scrap_a", [P, P])
        uT = sb("uT", [P, NB, SEQ])
        qT = sb("qT", [P, NB, SEQ])
        prob = sb("prob", [P, NT, GATES])
        pick = sb("pick", [P, NT, GATES])
        tmpg = sb("tmpg", [P, NT, GATES])
        gate = sb("gate", [P, NT, GATES])
        rank = sb("rank", [P, NE])
        NG = NT * 2 * NH
        top1 = sb("top1", [P, NG])
        top2 = sb("top2", [P, NG])
        topr = sb("topr", [P, NG])
        A = sb("A", [P, 2, NB, P])
        uTc = sb("uTc", [P, 2, NB, CHUNK])
        AuT = sb("AuT", [P, 2, NB, CHUNK])
        uA = sb("uA", [P, 2, P])
        M = sb("M", [P, 2, 2 * CHUNK])
        eye32 = sb("eye32", [P, CHUNK])
        nmask = sb("nmask", [P, CHUNK])
        nlow = sb("nlow", [P, P])
        row = sb("row", [P, 2, CHUNK + 1])
        rp = sb("rp", [P, 2])
        cf = sb("cf", [P, 2])
        Dv = sb("Dv", [P, 2])
        rD = sb("rD", [P, 2])
        rDf = sb("rDf", [P, 2])
        scr32 = sb("scr32", [P, CHUNK])
        Rbd = sb("Rbd", [P, 2, P])
        Wc = sb("Wc", [P, 2, P])
        Zc = sb("Zc", [P, 2, P])
        Zbd = sb("Zbd", [P, 2, NB, P])
        B0 = Zbd[:, 0, :, :]
        Y0 = Zbd[:, 1, :, :]
        own = sb("own", [P, NB])
        zT = sb("zT", [P, NB, SEQ])
        causal = sb("causal", [P, P])
        pT = sb("pT", [P, 2, 512])
        oT = sb("oT", [P, 512])
        qk_raw = sb("qk_raw", [P, 2, P])
        Ah = sb("Ah", [P, P], F32R)
        Al = sb("Al", [P, P], F32R)
        vo_raw = sb("vo_raw", [P, 2, NE * P])
        vo_h = sb("vo_h", [P, 2, NE * P], F32R)
        vo_l = sb("vo_l", [P, 2, NE * P], F32R)
        Th = sb("Th", [P, 512], F32R)
        Tl = sb("Tl", [P, 512], F32R)
        gh = sb("gh", [P, 2, NT, NE])
        goh = sb("goh", [P, 2, TB, NE])
        nmax = sb("nmax", [P, 2, TB])
        rsum = sb("rsum", [P, 2, TB])
        rinv = sb("rinv", [P, TB])
        prb = tmpg[:].rearrange("p a b -> p (a b)").rearrange("p (k n) -> p k n", k=TB)
        pTh = sb("pTh", [P, 2, 512], F32R)
        pTl = sb("pTl", [P, 2, 512], F32R)
        Va = sb("Va", [P, TB, P])
        Vb = sb("Vb", [P, TB, P])
        Vh = sb("Vh", [P, 512], F32R)
        Vl = sb("Vl", [P, 512], F32R)
        ch = sb("ch", [P, 512], F32R)
        cl = sb("cl", [P, 512], F32R)
        tmp = xn[:].rearrange("p (n e) d -> p n e d", e=GH)
        half = sb("half", [P, 2, P])
        quart = sb("quart", [P, P])
        both = sb("both", [P, GH, P])
        acc, acc2 = prob, pick

        id2 = sb("id2", [P, P])
        ida = sb("ida", [P, P])
        bS = [bank("bS0"), bank("bS1")]
        bPT = bank("bPT")
        bC = bank("bC")
        bY = [bank("bY0"), bank("bY1")]
        bG = bank("bG")
        bU = bank("bU")

        def sems(names):
            return [sem(n) for n in names.split()]

        ld_x, ld_w, ld_b, ld_qk, ld_vo, stored, zero_ok, ident_ok, pro_p = sems(
            "ld_x ld_w ld_b ld_qk ld_vo stored zero_ok ident_ok pro_p")
        var_ok, root_ok, xn_ok, kk_ok, kroot_ok, unit_ok, link_ok, gate_ok, acc_ok = sems(
            "var_ok root_ok xn_ok kk_ok kroot_ok unit_ok link_ok gate_ok acc_ok")
        xT_mm, xh_ok, xl_ok, wT_mm, wh_ok, wl_ok, qkv_mm, qkv_ok, lg_mm = sems(
            "xT_mm xh_ok xl_ok wT_mm wh_ok wl_ok qkv_mm qkv_ok lg_mm")
        lg_ok, ut_mm, ut_ok, c_uT, c_au, c_auE, c_g, c_fac, elim_ok = sems(
            "lg_ok ut_mm ut_ok c_uT c_au c_auE c_g c_fac elim_ok")
        n_mm, n_X, n_Y, c_Zbd, c_W, c_WE, c_z, c_zE, c_up, c_A, s_A, s_T, s_S = sems(
            "n_mm n_X n_Y c_Zbd c_W c_WE c_z c_zE c_up c_A s_A s_T s_S")
        s_Y0, s_Y1, s_PT, s_PV, a_A, d_A, a_wh, p_wl, a_T = sems(
            "s_Y0 s_Y1 s_PT s_PV a_A d_A a_wh p_wl a_T")
        d_T, d_max, a_exp, d_gate, d_gh, d_V, a_Vh, d_Vl, a_cp = sems(
            "d_T d_max a_exp d_gate d_gh d_V a_Vh d_Vl a_cp")
        p_half, p_quart, p_acc, a_PTh, d_PTl, a_C, d_C, d_rinv, d_goh = sems(
            "p_half p_quart p_acc a_PTh d_PTl a_C d_C d_rinv d_goh")
        f_p, f_diag, f_rest, f_o, f_oE, f_y, f_take, f_res = sems(
            "f_p f_diag f_rest f_o f_oE f_y f_take f_res")
        block = ctx.enter_context(nc.Block())

        x_v = x.rearrange("b (k p) d -> p (b k) d", p=P)
        out_v = out.rearrange("b (k p) d -> p (b k) d", p=P)
        qw_v = q_w.rearrange("(h p) d -> p h d", p=P)
        kw_v = k_w.rearrange("(h p) d -> p h d", p=P)
        vw_v = v_w.rearrange("(h e) d p -> d h e p", e=NE)
        ow_v = o_w.rearrange("(h e) p d -> p h e d", e=NE)

        def v_at(b, i):
            return i if b == 0 else 2 * TB * b - TB + i

        def o_at(b, j):
            return (2 * TB * (b + 1) if b < NB - 1 else 2 * TB * NB - TB) + j

        NEWTON = 11
        WORST = SEQ // 2 + 1
        ALPHA = 2.0 / (WORST + 1)
        STEPS = 2 * NB * TB

        def on_dve(n, g):
            tail = n >= STEPS - TB
            value = n < TB or (n < STEPS - TB and (n - TB) % (2 * TB) < TB)
            return g == 0 and (value or tail)

        DVE_AT = [sum(on_dve(m, 0) for m in range(n)) for n in range(STEPS + 1)]
        ND = DVE_AT[STEPS]
        NA = 2 * STEPS - ND

        def act_at(n, g):
            return 2 * n + g - DVE_AT[n] - (1 if g and on_dve(n, 0) else 0)

        HALVES_OF_HEAD = sum(1 if on_dve(n, 0) else 2 for n in range(STEPS))
        QUARTS = STEPS

        def taken(k):
            count, at, turn = 0, 0, 0
            if k < 0:
                k, turn = k + NA, HALVES_OF_HEAD
            for n in range(STEPS):
                count += 1
                at += 1 if on_dve(n, 0) else 2
                if k < at:
                    return count - turn
                count += 0 if on_dve(n, 0) else 1

        PHASES = (2 * NB + 1) * TB
        FACTOR_FROM = 2
        TWICE = range(TB, 2 * TB)

        def steps_of(ph):
            at = 0
            for p_ in range(FACTOR_FROM, ph + 1):
                m = 2 if p_ in TWICE else 1
                if p_ == ph:
                    return range(min(at, CHUNK - 1), min(at + m, CHUNK - 1))
                at += m
            return range(0)

        FACTORED = next(ph for ph in range(FACTOR_FROM, PHASES) if steps_of(ph) and steps_of(ph)[-1] == CHUNK - 2) + 1


        @block.sync
        def _(sp):
            for b in range(NB):
                sp.dma_start(x_sb[:, b * TB:(b + 1) * TB, :], x_v[:, b * TB:(b + 1) * TB, :]).then_inc(ld_x, 16)
            for n, w in enumerate((Wq, Wk, Wv, Wo)):
                sp.dma_start(w4[:, n, :], w).then_inc(ld_w, 16)
            sp.dma_start(sel[0:P // 2, :], sel_v_w).then_inc(ld_w, 16)
            sp.dma_start(sel[P // 2:P, :], sel_o_w).then_inc(ld_w, 16)
            for n, w in enumerate((bq, bk, bv)):
                sp.dma_start(bias3[:, n, :], w.rearrange("(a d) -> a d", a=1).broadcast_to([P, P])).then_inc(ld_b, 16)
            sp.dma_start(bo_b[:], bo.rearrange("(a d) -> a d", a=1).broadcast_to([P, P])).then_inc(ld_b, 16)
            sp.dma_start(rs_b[:], route_scale.rearrange("(a d) -> a d", a=1).broadcast_to([P, 1])).then_inc(ld_b, 16)
            def load_qk(h):
                sp.dma_start(qk_raw[:, 0, :], qw_v[:, bass.ds(h, 1), :].rearrange("p a d -> p (a d)")).then_inc(ld_qk, 16)
                sp.dma_start(qk_raw[:, 1, :], kw_v[:, bass.ds(h, 1), :].rearrange("p a d -> p (a d)")).then_inc(ld_qk, 16)

            def load_vo(h):
                sp.dma_start(vo_raw[:, 0, :].rearrange("p (e d) -> p e d", e=NE),
                             vw_v[:, bass.ds(h, 1), :, :].rearrange("p a e d -> p (a e) d")).then_inc(ld_vo, 16)
                sp.dma_start(vo_raw[:, 1, :].rearrange("p (e d) -> p e d", e=NE),
                             ow_v[:, bass.ds(h, 1), :, :].rearrange("p a e d -> p (a e) d")).then_inc(ld_vo, 16)

            load_qk(0)
            load_vo(0)
            with sp.Fori(1, NH) as h:
                sp.wait_ge(s_A, h)
                load_qk(h)
                sp.wait_ge(a_wh, h * 2)
                sp.wait_ge(p_wl, h * 2)
                load_vo(h)
            for b in range(NB):
                sp.wait_ge(f_res, b + 1)
                sp.dma_start(out_v[:, b * TB:(b + 1) * TB, :], x_sb[:, b * TB:(b + 1) * TB, :]).then_inc(stored, 16)
            sp.wait_ge(stored, 16 * NB)

        @block.gpsimd
        def _(pool):
            for started in (p_quart, p_acc, p_half):
                pool.sem_inc(started, FIRST)
            g = nc.gpsimd
            g.memset(ident[:], 0.0).then_inc(pro_p, 1)
            g.memset(nlow[:], -1.0).then_inc(pro_p, 1)
            g.memset(causal[:], 1.0).then_inc(pro_p, 1)
            pool.wait_ge(pro_p, 3)
            g.affine_select(out=ident[:], in_=ident[:], compare_op=ALU.not_equal, fill=1.0, base=0,
                            pattern=[[-1, P]], channel_multiplier=1).then_inc(ident_ok, 1)
            g.affine_select(out=nlow[:], in_=nlow[:], compare_op=ALU.is_gt, fill=0.0, base=0,
                            pattern=[[-1, P]], channel_multiplier=1).then_inc(ident_ok, 1)
            g.affine_select(out=causal[:], in_=causal[:], compare_op=ALU.is_ge, fill=0.0, base=0,
                            pattern=[[1, P]], channel_multiplier=-1).then_inc(ident_ok, 1)
            for e in range(NE):
                g.memset(rank[:, e:e + 1], float(NE - e)).then_inc(zero_ok, 1)
            g.memset(Rbd[:], 0.0).then_inc(zero_ok, 1)
            pool.wait_ge(gate_ok, 1)
            g.memset(acc[:], 0.0).then_inc(acc_ok, 1)
            g.memset(acc2[:], 0.0).then_inc(acc_ok, 1)
            pool.wait_ge(acc_ok, 2)

            with pool.Fori(0, NH) as h:
                for n in range(2):
                    pool.wait_ge(a_wh, h * 2 + n + 1)
                    g.tensor_tensor(vo_l[:, n, :], vo_raw[:, n, :], vo_h[:, n, :].bitcast(F32), ALU.subtract).then_inc(p_wl, 1)

                HALF0, OUT0 = h * HALVES_OF_HEAD, h * (NB * TB)
                halves, quarts = [0], [0]

                def halve(in_, k):
                    pool.wait_ge(p_quart, FIRST + h * QUARTS + quarts[0])
                    g.tensor_tensor(half[:], in_[:, 0:2, :], in_[:, 2:4, :], ALU.add).then_inc(p_half, 1)
                    halves[0] += 1
                    pool.wait_ge(p_half, FIRST + HALF0 + halves[0])

                def value(b, i):
                    k = act_at(v_at(b, i), 1)
                    pool.wait_ge(a_cp, FIRST + h * (GH * NA) + GH * (k + 1))
                    halve(tmp[:, k % 4, :, :], k)
                    g.tensor_tensor(Vb[:, i, :], half[:, 0, :], half[:, 1, :], ALU.add).then_inc(p_quart, 1)
                    quarts[0] += 1

                def output(b, j):
                    n = o_at(b, j)
                    k = act_at(n, 1)
                    pool.wait_ge(a_cp, FIRST + h * (GH * NA) + GH * (k + 1))
                    if on_dve(n, 0):
                        halve(tmp[:, k % 4, :, :], k)
                    else:
                        pool.wait_ge(p_half, FIRST + HALF0 + halves[0])
                        g.tensor_tensor(both[:], tmp[:, (k - 1) % 4, :, :], tmp[:, k % 4, :, :], ALU.add).then_inc(p_half, 1)
                        halves[0] += 1
                        pool.wait_ge(p_half, FIRST + HALF0 + halves[0])
                        halve(both[:], k)
                    pool.wait_ge(p_acc, FIRST + OUT0 + b * TB + j)
                    g.tensor_tensor(quart[:], half[:, 0, :], half[:, 1, :], ALU.add).then_inc(p_quart, 1)
                    quarts[0] += 1
                    pool.wait_ge(p_quart, FIRST + h * QUARTS + quarts[0])
                    m = b * TB + j
                    g.tensor_tensor(acc2[:, m, :], acc2[:, m, :], quart[:], ALU.add).then_inc(p_acc, 1)

                for b in range(NB):
                    pool.wait_ge(d_V, FIRST + h * NB + b)
                    for i in range(TB):
                        value(b, i)
                    for j in range(TB):
                        if b:
                            output(b - 1, j)
                        if b == NB - 1 and j == TB - 1:
                            for f in range(2):
                                pool.wait_ge(c_WE, h * 3 + 2 + f)
                                g.tensor_tensor(Zbd[:, f, :, :], Zc[:, f, :].rearrange("p (a d) -> p a d", a=1).broadcast_to([P, NB, P]),
                                                own[:].rearrange("p (b a) -> p b a", a=1).broadcast_to([P, NB, P]), ALU.mult).then_inc(c_Zbd, 1)
                for j in range(TB):
                    output(NB - 1, j)

        @block.tensor
        def _(pe):
            for started in (c_g, s_Y0, s_Y1, s_PV):
                pe.sem_inc(started, FIRST)
            t = nc.tensor

            def mm3(out_, ah, al, bh, bl, start=True, stop=True):
                t.matmul(out_, ah, bh, start=start, stop=False)
                t.matmul(out_, ah, bl, start=False, stop=False)
                return t.matmul(out_, al, bh, start=False, stop=stop)

            pe.wait_ge(ident_ok, 1)
            pe.wait_ge(ld_w, 96)
            for n in range(4):
                t.transpose(bY[0][:, n * P:(n + 1) * P], w4[:, n, :], ident[:]).then_inc(wT_mm, 1)
            t.transpose(bY[1][:, 0:P], sel[:], ident[:]).then_inc(wT_mm, 1)
            for b in range(NB):
                pe.wait_ge(xn_ok, b + 1)
                if b >= 2:
                    pe.wait_ge(xl_ok, b - 1)
                for i in range(TB):
                    q = t.transpose(bS[b % 2][:, i * P:(i + 1) * P], xn[:, b * TB + i, :], ident[:])
                q.then_inc(xT_mm, 1)
            pe.wait_ge(wh_ok, 3)
            pe.wait_ge(wl_ok, 2)
            for k in range(NT):
                pe.wait_ge(xh_ok, k // TB + 1)
                pe.wait_ge(xl_ok, k // TB + 1)
                c = slice(k * P, (k + 1) * P)
                if k % TB == 0 and k >= 2 * TB:
                    pe.wait_ge(lg_ok, k // TB - 1)
                q = mm3(bY[k // TB % 2][:, k % TB * P:(k % TB + 1) * P], xh[:, c], xl[:, c], selh[:], sell[:])
                if k % TB == TB - 1:
                    q.then_inc(lg_mm, 1)
                if k >= 2:
                    pe.wait_ge(qkv_ok, k - 1)
                mm3((bG, bU)[k % 2][:, 0:3 * P], xh[:, c], xl[:, c], w3h[:], w3l[:]).then_inc(qkv_mm, 1)
            for n in range(2 * NB):
                b = n % NB
                pe.wait_ge(unit_ok, 1)
                if n >= 2:
                    pe.wait_ge(ut_ok, n - 1)
                for i in range(TB):
                    q = t.transpose(bS[n % 2][:, i * P:(i + 1) * P], qkv[:, b * TB + i, 1 if n < NB else 0, :], ident[:])
                q.then_inc(ut_mm, 1)

            for b in range(NB):
                for k in range(TB // 2):
                    u = qkv[:, b * TB + k, 1, :]
                    q = t.matmul(bC[:, b * P:(b + 1) * P], u, u, start=(k == 0), stop=(k == TB // 2 - 1))
            q.then_inc(n_mm, 1)
            for n in range(NEWTON):
                pe.wait_ge(n_X, n + 1)
                for b in range(NB):
                    q = t.matmul(bPT[:, b * P:(b + 1) * P], B0[:, b, :], A[:, 1, b, :], start=True, stop=True)
                q.then_inc(n_mm, 1)
                pe.wait_ge(n_Y, n + 1)
                for b in range(NB):
                    q = t.matmul(bC[:, b * P:(b + 1) * P], A[:, 1, b, :], Y0[:, b, :], start=True, stop=True)
                q.then_inc(n_mm, 1)

            pe.wait_ge(n_X, NEWTON + 1)
            with pe.Fori(0, NH) as h:
                def expert(side, n, lh, ll):
                    for g, ready in enumerate((s_Y0, s_Y1)):
                        e = slice(g * 512, (g + 1) * 512)
                        if on_dve((n - 1) % STEPS, g):
                            pe.wait_ge(d_gate, FIRST + h * (GH * ND) + GH * DVE_AT[n])
                        else:
                            pe.wait_ge(a_cp, FIRST + h * (GH * NA) + GH * (act_at(n - 1, g) + 1 if n else 0))
                        mm3(bY[g][:], lh, ll, vo_h[:, side, e], vo_l[:, side, e]).then_inc(ready, 1)

                def project(b):
                    c = slice(b * 512, (b + 1) * 512)
                    mm3(bS[0][:], Ah[:], Al[:], xh[:, c], xl[:, c]).then_inc(s_T, 1)

                def output(b, j):
                    c = slice(j * P, (j + 1) * P)
                    if j == 0:
                        pe.wait_ge(a_C, h * NB + b + 1)
                        pe.wait_ge(d_C, FIRST + h * NB + b + 1)
                    expert(1, o_at(b, j), ch[:, c], cl[:, c])

                def rec_au():
                    pe.wait_ge(c_uT, h * 2 + 2)
                    pe.wait_ge(c_zE, FIRST + h * 2)
                    for f in range(2):
                        for b in range(NB):
                            m = (f * NB + b) * CHUNK
                            t.matmul(bG[:, m:m + CHUNK], A[:, f, b, :], uTc[:, f, b, :], start=True, stop=True)
                    for f in range(2):
                        for b in range(NB):
                            q = t.matmul(bG[b * CHUNK:(b + 1) * CHUNK, 2 * P + f * P:3 * P + f * P], uTc[:, f, b, :], A[:, f, b, :],
                                         start=True, stop=True)
                    q.then_inc(c_au, 1)

                def rec_gram():
                    pe.wait_ge(c_auE, h * 2 + 2)
                    for f in range(2):
                        for b in range(NB):
                            q = t.matmul(bG[b * CHUNK:(b + 1) * CHUNK, f * CHUNK:(f + 1) * CHUNK], uTc[:, f, b, :], AuT[:, f, b, :],
                                         start=True, stop=True)
                    q.then_inc(c_g, 1)

                def rec_w():
                    pe.wait_ge(c_fac, h + 1)
                    for f in range(2):
                        q = t.matmul(bG[:, 2 * P + f * P:3 * P + f * P], Rbd[:, f, :], uA[:, f, :], start=True, stop=True)
                    q.then_inc(c_W, 1)

                def rec_update():
                    pe.wait_ge(c_Zbd, h * 2 + 2)
                    for f, into in enumerate((bU, bC)):
                        t.matmul(into[:], Wc[:, f, :], Zbd[:, f, :, :].rearrange("p b d -> p (b d)"), start=True, stop=True).then_inc(c_up, 1)
                    for f in range(2):
                        q = t.transpose(bG[:, f * P:(f + 1) * P], Zc[:, f, :], ident[:])
                    q.then_inc(c_z, 1)

                pe.wait_ge(ld_qk, h * 32 + 32)
                pe.wait_ge(d_C, FIRST + h * NB)
                pe.wait_ge(c_A, h * 2 + 1)
                t.matmul(bC[:, 0:P], qk_raw[:, 0, :], qk_raw[:, 1, :], start=True, stop=True).then_inc(s_A, 1)
                pe.wait_ge(a_A, h + 1)
                pe.wait_ge(d_A, h + 1)
                project(0)
                pe.wait_ge(a_wh, h * 2 + 2)
                pe.wait_ge(p_wl, h * 2 + 2)
                for b in range(NB):
                    pe.wait_ge(a_T, h * NB + b + 1)
                    pe.wait_ge(d_T, h * NB + b + 1)
                    for i in range(TB):
                        c = slice(i * P, (i + 1) * P)
                        kc = slice(b * 512, (b + 1) * 512)
                        if i >= 2:
                            pe.wait_ge(a_exp, h * NB * TB + b * TB + i - 1)
                        mm3(bS[i % 2][:], Th[:, c], Tl[:, c], xh[:, kc], xl[:, kc]).then_inc(s_S, 1)
                        xc = slice((b * TB + i) * P, (b * TB + i + 1) * P)
                        expert(0, v_at(b, i), xh[:, xc], xl[:, xc])
                        if b == 0 and i == 0:
                            rec_au()
                        if b == 0 and i == 1:
                            rec_gram()
                    pe.wait_ge(a_exp, h * NB * TB + (b + 1) * TB)
                    if b < NB - 1:
                        project(b + 1)
                    for j in range(TB):
                        n = h * NB * TB + b * TB + j
                        pe.wait_ge(d_PTl, FIRST + n)
                        for i in range(TB):
                            q = t.transpose(bPT[:, i * P:(i + 1) * P], prb[:, i, j * P:(j + 1) * P], ident[:])
                        q.then_inc(s_PT, 1)
                        if b:
                            output(b - 1, j)
                        if j == 0:
                            pe.wait_ge(a_Vh, h * NB + b + 1)
                            pe.wait_ge(d_Vl, h * NB + b + 1)
                            if b:
                                pe.wait_ge(d_C, FIRST + h * NB + b)
                        pe.wait_ge(d_PTl, FIRST + n + 1)
                        vc = slice(j * P, (j + 1) * P)
                        mm3(bC[:], Vh[:, vc], Vl[:, vc], pTh[:, j % 2, :], pTl[:, j % 2, :],
                            start=(j == 0), stop=(j == TB - 1)).then_inc(s_PV, 1)
                        if b * 2 * TB + TB + j == FACTORED + 1:
                            rec_w()
                for j in range(TB):
                    output(NB - 1, j)
                    if j == 1:
                        rec_update()

            pe.wait_ge(c_zE, FIRST + NH * 2)
            def rest(n):
                return n // TB * (TB - 1) + min(n % TB + 1, TB - 1)

            for b in range(NB):
                def weigh(i):
                    n = b * TB + i
                    pe.wait_ge(f_diag, n + 1)
                    pe.wait_ge(f_rest, rest(n))
                    if i == 0 and b:
                        pe.wait_ge(f_oE, b)
                    t.matmul(bC[:, i * P:], qkv[:, n, 2, :], pT[:, i % 2, 0:SEQ - i * P],
                             start=(i == 0), stop=(i == TB - 1)).then_inc(f_o, 1)

                for i in range(TB):
                    n = b * TB + i
                    if n >= 2:
                        pe.wait_ge(f_diag, n - 1)
                        pe.wait_ge(f_rest, rest(n - 2))
                    t.matmul(bS[i % 2][:, 0:SEQ - i * P], zT[:, b, i * P:(i + 1) * P], qT[:, b, i * P:],
                             start=True, stop=True).then_inc(f_p, 1)
                    if i:
                        weigh(i - 1)
                weigh(TB - 1)
                pe.wait_ge(f_oE, b + 1)
                pe.wait_ge(f_take, b) if b else None
                for i in range(TB):
                    q = t.matmul(bPT[:, i * P:(i + 1) * P], oT[:, i * P:(i + 1) * P], woT[:], start=True, stop=True)
                q.then_inc(f_y, 1)

        @block.scalar
        def _(act):
            for started in (a_cp, c_zE):
                act.sem_inc(started, FIRST)
            a = nc.scalar
            act.wait_ge(var_ok, 1)
            a.activation(small_a[:], rstd[:], ACT.Sqrt).then_inc(root_ok, 1)
            act.wait_ge(wT_mm, 5)
            a.activation(w3h[:], bY[0][:, 0:3 * P], ACT.Copy).then_inc(wh_ok, 1)
            a.activation(woT[:], bY[0][:, 3 * P:], ACT.Copy).then_inc(wh_ok, 1)
            a.activation(selh[:], bY[1][:, 0:P], ACT.Copy).then_inc(wh_ok, 1)
            for b in range(NB):
                act.wait_ge(xT_mm, b + 1)
                a.activation(xh[:, b * 512:(b + 1) * 512], bS[b % 2][:], ACT.Copy).then_inc(xh_ok, 1)
            for b in range(NB):
                act.wait_ge(lg_mm, b + 1)
                a.activation(prob[:, b * TB:(b + 1) * TB, :].rearrange("p a b -> p (a b)"), bY[b % 2][:], ACT.Exp, scale=-1.0).then_inc(lg_ok, 1)
            act.wait_ge(kk_ok, 1)
            a.activation(small_b[:], kk[:], ACT.Sqrt).then_inc(kroot_ok, 1)
            for n in range(2 * NB):
                act.wait_ge(ut_mm, n + 1)
                a.activation((uT if n < NB else qT)[:, n % NB, :], bS[n % 2][:], ACT.Copy).then_inc(ut_ok, 1)

            for n in range(NEWTON):
                act.wait_ge(n_mm, 2 * n + 3)
                a.activation(A[:, 1, :, :].rearrange("p b d -> p (b d)"), bC[:], ACT.Copy).then_inc(n_X, 1)

            with act.Fori(0, NH) as h:
                A0 = h * (GH * NA)
                act.wait_ge(ut_ok, 2 * NB)
                act.wait_ge(c_g, FIRST + h)
                for f in range(2):
                    a.activation(uTc[:, f, :, :], uT[:, :, bass.ds(f * (SEQ // 2) + h * CHUNK, CHUNK)], ACT.Copy).then_inc(c_uT, 1)

                def scaled(n, g, g4, k):
                    act.wait_ge((s_Y0, s_Y1)[g], FIRST + h * STEPS + n + 1)
                    m = act_at(n, g)
                    act.wait_ge(p_half, FIRST + h * HALVES_OF_HEAD + taken(m - 4))
                    for e in range(GH):
                        a.activation(tmp[:, m % 4, e, :], bY[g][:, e * P:(e + 1) * P], ACT.Copy,
                                     scale=g4[:, k, g * GH + e:g * GH + e + 1]).then_inc(a_cp, 1)

                def output(b, j):
                    n = o_at(b, j)
                    for g in range(2):
                        if not on_dve(n, g):
                            scaled(n, g, goh[:, b % 2, :, :], j)

                def project(b):
                    act.wait_ge(s_T, h * NB + b + 1)
                    a.activation(Th[:], bS[0][:], ACT.Copy).then_inc(a_T, 1)

                act.wait_ge(s_A, h + 1)
                a.activation(Ah[:], bC[:, 0:P], ACT.Copy, scale=SCALE).then_inc(a_A, 1)
                act.wait_ge(ld_vo, h * 32 + 32)
                for n in range(2):
                    act.wait_ge(s_Y1, FIRST + h * STEPS)
                    a.activation(vo_h[:, n, :], vo_raw[:, n, :], ACT.Copy).then_inc(a_wh, 1)
                project(0)
                act.wait_ge(d_gh, h * 2 + 2)
                for b in range(NB):
                    for i in range(TB):
                        n = h * NB * TB + b * TB + i
                        act.wait_ge(d_max, n + 1)
                        a.activation(prb[:, i, :], bS[i % 2][:], ACT.Exp, bias=nmax[:, b % 2, i:i + 1],
                                     accum_out=rsum[:, b % 2, i:i + 1]).then_inc(a_exp, 1)
                        scaled(v_at(b, i), 1, gh[:, 0, :, :], b * TB + i)
                        if b == 0 and i == 0:
                            act.wait_ge(c_au, h + 1)
                            a.activation(AuT[:].rearrange("p f b d -> p (f b d)"), bG[:, 0:2 * P], ACT.Copy).then_inc(c_auE, 1)
                            a.activation(uA[:].rearrange("p f d -> p (f d)"), bG[:, 2 * P:], ACT.Copy).then_inc(c_auE, 1)
                    if b < NB - 1:
                        project(b + 1)
                    for j in range(TB):
                        n = h * NB * TB + b * TB + j
                        act.wait_ge(s_PT, n + 1)
                        if j == 0:
                            act.wait_ge(s_PV, FIRST + h * NB * TB + b * TB)
                        if j >= 2:
                            act.wait_ge(s_PV, FIRST + n - 1)
                        a.activation(pTh[:, j % 2, :], bPT[:], ACT.Copy).then_inc(a_PTh, 1)
                        if j == 0:
                            act.wait_ge(d_V, FIRST + h * NB + b + 1)
                            a.activation(Vh[:], Va[:].rearrange("p b d -> p (b d)"), ACT.Copy).then_inc(a_Vh, 1)
                        if b:
                            if j == 0:
                                act.wait_ge(d_goh, h * NB + b)
                            output(b - 1, j)
                        if b * 2 * TB + TB + j == FACTORED + 1:
                            act.wait_ge(c_W, h + 1)
                            a.activation(Wc[:].rearrange("p f d -> p (f d)"), bG[:, 2 * P:], ACT.Copy).then_inc(c_WE, 1)
                            for f in range(2):
                                a.activation(Zc[:, f, :], bG[:, 2 * P + f * P:3 * P + f * P], ACT.Copy, scale=rDf[:, f:f + 1]).then_inc(c_WE, 1)
                    act.wait_ge(s_PV, FIRST + h * NB * TB + (b + 1) * TB)
                    a.activation(ch[:], bC[:], ACT.Copy).then_inc(a_C, 1)
                act.wait_ge(d_goh, h * NB + NB)
                for j in range(TB):
                    output(NB - 1, j)
                act.wait_ge(c_z, h + 1)
                for f in range(2):
                    a.activation(zT[:, :, bass.ds(f * (SEQ // 2) + h * CHUNK, CHUNK)],
                                 bG[:, f * P:(f + 1) * P].rearrange("p (b d) -> p b d", b=NB), ACT.Copy).then_inc(c_zE, 1)

            for b in range(NB):
                for i in range(TB - 1):
                    act.wait_ge(f_diag, b * TB + i + 1)
                    w = SEQ - i * P
                    a.activation(pT[:, i % 2, P:w], bS[i % 2][:, P:w], ACT.Copy).then_inc(f_rest, 1)
                act.wait_ge(f_o, (b + 1) * TB)
                a.activation(oT[:], bC[:], ACT.Copy).then_inc(f_oE, 1)

        @block.vector
        def _(dve):
            for started in (d_V, d_gate, d_C, d_PTl):
                dve.sem_inc(started, FIRST)
            v = nc.vector
            linked = [0]

            def link(ins):
                linked[0] += 1
                ins.then_inc(link_ok, 1)
                dve.wait_ge(link_ok, linked[0])

            def wide(g2):
                return g2[:].rearrange("p (g a) -> p g a", a=1).broadcast_to([P, NG, NE])

            def grouped(g3):
                return g3[:].rearrange("p k (g e) -> p (k g) e", e=NE)

            dve.wait_ge(ld_x, 16 * NB)
            for k in range(NT):
                q = v.bn_stats(stats[:, k, :], x_sb[:, k, :])
            link(q)
            for k in range(NT):
                q = v.bn_aggr(mv[:, k, :], stats[:, k, :])
            link(q)
            v.tensor_scalar(rstd[:], mv[:, :, 1], LN_EPS, None, ALU.add).then_inc(var_ok, 1)
            dve.wait_ge(root_ok, 1)
            dve.wait_ge(var_ok, 1)
            link(v.reciprocal(small_b[:], small_a[:]))
            link(v.tensor_tensor(small_a[:], small_b[:], small_b[:], ALU.mult))
            link(v.tensor_tensor(small_a[:], small_a[:], rstd[:], ALU.mult))
            link(v.tensor_scalar(small_a[:], small_a[:], -0.5, 1.5, ALU.mult, ALU.add))
            link(v.tensor_tensor(rstd[:], small_a[:], small_b[:], ALU.mult))
            for k in range(NT):
                q = v.tensor_scalar(xn[:, k, :], x_sb[:, k, :], mv[:, k, 0:1], rstd[:, k:k + 1], ALU.subtract, ALU.mult)
                if k % TB == TB - 1:
                    q.then_inc(xn_ok, 1)
            dve.wait_ge(wh_ok, 3)
            v.tensor_tensor(w3l[:], bY[0][:, 0:3 * P], w3h[:].bitcast(F32), ALU.subtract).then_inc(wl_ok, 1)
            v.tensor_tensor(sell[:], bY[1][:, 0:P], selh[:].bitcast(F32), ALU.subtract).then_inc(wl_ok, 1)
            for b in range(NB):
                dve.wait_ge(xh_ok, b + 1)
                c = slice(b * 512, (b + 1) * 512)
                v.tensor_tensor(xl[:, c], bS[b % 2][:], xh[:, c].bitcast(F32), ALU.subtract).then_inc(xl_ok, 1)
            dve.wait_ge(ld_b, 80)
            for k in range(NT):
                dve.wait_ge(qkv_mm, k + 1)
                v.tensor_tensor(qkv[:, k, :, :], (bG, bU)[k % 2][:, 0:3 * P].rearrange("p (a b) -> p a b", a=3),
                                bias3[:], ALU.add).then_inc(qkv_ok, 1)
            dve.wait_ge(qkv_ok, NT)
            for k in range(NT):
                link(v.tensor_tensor_reduce(scrap_v[:], qkv[:, k, 0, :], qkv[:, k, 1, :], 1.0, 0.0, ALU.mult, ALU.add, kq[:, k:k + 1]))
            for k in range(NT):
                link(v.tensor_tensor_reduce(scrap_v[:], qkv[:, k, 1, :], qkv[:, k, 1, :], 1.0, 0.0, ALU.mult, ALU.add, kk[:, k:k + 1]))
            v.tensor_scalar(kk[:], kk[:], 1.0, None, ALU.mult).then_inc(kk_ok, 1)
            dve.wait_ge(kk_ok, 1)
            dve.wait_ge(kroot_ok, 1)
            link(v.tensor_scalar(small_a[:], small_b[:], TINY, None, ALU.max))
            link(v.reciprocal(small_a[:], small_a[:]))
            link(v.tensor_tensor(small_a[:], small_a[:], kk[:], ALU.mult))
            link(v.tensor_tensor(small_a[:], small_a[:], small_b[:], ALU.add))
            link(v.tensor_scalar(small_a[:], small_a[:], 0.5, NORM_EPS, ALU.mult, ALU.add))
            link(v.reciprocal(kn[:], small_a[:]))
            for k in range(NT):
                v.tensor_scalar(qkv[:, k, 1, :], qkv[:, k, 1, :], kn[:, k:k + 1], None, ALU.mult)
                q = v.tensor_scalar(qkv[:, k, 2, :], qkv[:, k, 2, :], kq[:, k:k + 1], None, ALU.mult)
            q.then_inc(unit_ok, 1)
            dve.wait_ge(ident_ok, 3)
            for b in range(NB):
                r = slice(b * CHUNK, (b + 1) * CHUNK)
                link(v.tensor_copy(eye32[r, :], ident[r, r]))
                link(v.tensor_copy(nmask[r, :], nlow[r, r]))
            link(v.tensor_reduce(own[:], ident[:].rearrange("p (b k) -> p b k", b=NB), AX_X, ALU.add))
            link(v.tensor_scalar(id2[:], ident[:], 2.0, None, ALU.mult))
            link(v.tensor_scalar(ida[:], ident[:], 2.0 * ALPHA, None, ALU.mult))
            for b in range(NB):
                link(v.tensor_copy(A[:, 0, b, :], ident[:]))
            each = ident[:].rearrange("p (a d) -> p a d", a=1).broadcast_to([P, NB, P])
            dve.wait_ge(n_mm, 1)
            link(v.tensor_tensor(B0, bC[:].rearrange("p (b d) -> p b d", b=NB), each, ALU.add))
            v.scalar_tensor_tensor(out=A[:, 1, :, :], in0=B0, scalar=-ALPHA * ALPHA,
                                   in1=ida[:].rearrange("p (a d) -> p a d", a=1).broadcast_to([P, NB, P]),
                                   op0=ALU.mult, op1=ALU.add).then_inc(n_X, 1)
            newtons = [0]

            def newton():
                dve.wait_ge(n_mm, 2 * newtons[0] + 2)
                v.scalar_tensor_tensor(out=Y0, in0=bPT[:].rearrange("p (b d) -> p b d", b=NB), scalar=-1.0,
                                       in1=id2[:].rearrange("p (a d) -> p a d", a=1).broadcast_to([P, NB, P]),
                                       op0=ALU.mult, op1=ALU.add).then_inc(n_Y, 1)
                newtons[0] += 1

            dve.wait_ge(lg_ok, NB)
            dve.wait_ge(zero_ok, NE + 1)
            link(v.tensor_scalar(prob[:], prob[:], 1.0, None, ALU.add))
            newton()
            link(v.reciprocal(prob[:], prob[:]))
            ranks = rank[:].rearrange("p (a e) -> p a e", a=1).broadcast_to([P, NG, NE])
            link(v.tensor_reduce(top1[:], grouped(prob), AX_X, ALU.max))
            newton()
            link(v.tensor_tensor(grouped(pick), grouped(prob), wide(top1), ALU.is_equal))
            newton()
            link(v.tensor_tensor(grouped(pick), grouped(pick), ranks, ALU.mult))
            link(v.tensor_reduce(topr[:], grouped(pick), AX_X, ALU.max))
            newton()
            link(v.tensor_tensor(grouped(pick), grouped(pick), wide(topr), ALU.is_equal))
            newton()
            link(v.scalar_tensor_tensor(out=tmpg[:], in0=pick[:], scalar=-2.0, in1=prob[:], op0=ALU.mult, op1=ALU.add))
            link(v.tensor_reduce(top2[:], grouped(tmpg), AX_X, ALU.max))
            newton()
            link(v.tensor_tensor(grouped(tmpg), grouped(tmpg), wide(top2), ALU.is_equal))
            link(v.tensor_tensor(grouped(tmpg), grouped(tmpg), ranks, ALU.mult))
            newton()
            link(v.tensor_reduce(topr[:], grouped(tmpg), AX_X, ALU.max))
            newton()
            link(v.tensor_tensor(grouped(tmpg), grouped(tmpg), wide(topr), ALU.is_equal))
            link(v.tensor_tensor(pick[:], pick[:], tmpg[:], ALU.add))
            newton()
            link(v.tensor_tensor(gate[:], pick[:], prob[:], ALU.mult))
            link(v.tensor_tensor(topr[:], top1[:], top2[:], ALU.add))
            newton()
            link(v.tensor_scalar(topr[:], topr[:], 1e-9, None, ALU.max))
            newton()
            link(v.reciprocal(topr[:], topr[:]))
            link(v.tensor_scalar(topr[:], topr[:], rs_b[:, 0:1], None, ALU.mult))
            link(v.tensor_tensor(grouped(gate), grouped(gate), wide(topr), ALU.mult))
            v.tensor_scalar(rs_b[:], rs_b[:], 1.0, None, ALU.mult).then_inc(gate_ok, 1)
            dve.wait_ge(n_Y, NEWTON)
            v.tensor_copy(scrap_v[:, 0:1], kn[:, 0:1]).then_inc(c_A, 1)

            with dve.Fori(0, NH) as h:
                dve.sem_clear(elim_ok)

                def build():
                    dve.wait_ge(c_g, FIRST + h + 1)
                    v.tensor_tensor(M[:, :, 0:CHUNK], bG[:, 0:2 * CHUNK].rearrange("p (f k) -> p f k", f=2),
                                    eye32[:].rearrange("p (a k) -> p a k", a=1).broadcast_to([P, 2, CHUNK]), ALU.add).then_inc(elim_ok, 1)
                    v.tensor_copy(M[:, :, CHUNK:], eye32[:].rearrange("p (a k) -> p a k", a=1).broadcast_to([P, 2, CHUNK])).then_inc(elim_ok, 1)

                def eliminate(k, part):
                    at = 2 + 5 * k + part
                    dve.wait_ge(elim_ok, at if part < 4 else at - 1)
                    if part == 0:
                        q = v.stream_shuffle(row[:], M[:, :, k:k + CHUNK + 1], [k] * CHUNK)
                    elif part == 1:
                        q = v.reciprocal(rp[:], row[:, :, 0])
                    elif part == 2:
                        q = v.scalar_tensor_tensor(out=cf[:], in0=M[:, :, k], scalar=nmask[:, k:k + 1], in1=rp[:], op0=ALU.mult, op1=ALU.mult)
                    else:
                        f = part - 3
                        w = M[:, f, k + 1:k + CHUNK + 1]
                        q = v.scalar_tensor_tensor(out=w, in0=row[:, f, 1:], scalar=cf[:, f:f + 1], in1=w, op0=ALU.mult, op1=ALU.add)
                    q.then_inc(elim_ok, 1)

                def finish_factor():
                    at = 2 + 5 * (CHUNK - 1)
                    dve.wait_ge(elim_ok, at)
                    for f in range(2):
                        if f:
                            dve.wait_ge(elim_ok, at + f)
                        v.tensor_tensor_reduce(scr32[:], M[:, f, 0:CHUNK], eye32[:], 1.0, 0.0, ALU.mult, ALU.add, Dv[:, f:f + 1]).then_inc(elim_ok, 1)
                    for f in range(2):
                        for b in range(NB):
                            r = slice(b * CHUNK, (b + 1) * CHUNK)
                            v.transpose(Rbd[r, f, r], M[r, f, CHUNK:]).then_inc(elim_ok, 1)
                    dve.wait_ge(elim_ok, at + 2)
                    v.reciprocal(rDf[:], Dv[:]).then_inc(c_fac, 1)

                def parts_of(ph):
                    return [(k, part) for k in steps_of(ph) for part in range(5)]

                def gated(n, into, g4, k, fresh, between):
                    dve.wait_ge(s_Y0, FIRST + h * STEPS + n + 1)
                    for e in range(GH):
                        dve.wait_ge(d_gate, FIRST + h * (GH * ND) + GH * DVE_AT[n] + e)
                        y, g1 = bY[0][:, e * P:(e + 1) * P], g4[:, k, e:e + 1]
                        if fresh and e == 0:
                            q = v.tensor_scalar(into, y, g1, None, ALU.mult)
                        else:
                            q = v.scalar_tensor_tensor(out=into, in0=y, scalar=g1, in1=into, op0=ALU.mult, op1=ALU.add)
                        q.then_inc(d_gate, 1)
                        for m in range(e * len(between) // GH, (e + 1) * len(between) // GH):
                            eliminate(*between[m])

                def project(b):
                    dve.wait_ge(a_T, h * NB + b + 1)
                    v.tensor_tensor(Tl[:], bS[0][:], Th[:].bitcast(F32), ALU.subtract).then_inc(d_T, 1)

                def output(b, j, between):
                    if on_dve(o_at(b, j), 0):
                        dve.wait_ge(d_goh, h * NB + b + 1)
                        gated(o_at(b, j), acc[:, b * TB + j, :], goh[:, b % 2, :, :], j, False, between)
                    else:
                        for part in between:
                            eliminate(*part)

                dve.wait_ge(acc_ok, 2)
                dve.wait_ge(a_A, h + 1)
                v.scalar_tensor_tensor(out=Al[:], in0=bC[:, 0:P], scalar=SCALE, in1=Ah[:].bitcast(F32),
                                       op0=ALU.mult, op1=ALU.subtract).then_inc(d_A, 1)
                dve.wait_ge(a_cp, FIRST + h * (GH * NA))
                dve.wait_ge(d_gate, FIRST + h * (GH * ND))
                v.tensor_copy(gh[:, 0, :, :], gate[:, :, bass.ds(h * NE, NE)]).then_inc(d_gh, 1)
                v.tensor_copy(gh[:, 1, :, :], gate[:, :, bass.ds(NH * NE + h * NE, NE)]).then_inc(d_gh, 1)
                project(0)
                dve.wait_ge(d_gh, h * 2 + 2)
                for b in range(NB):
                    for i in range(TB):
                        n = h * NB * TB + b * TB + i
                        ph = b * 2 * TB + i
                        dve.wait_ge(s_S, n + 1)
                        v.tensor_reduce(nmax[:, b % 2, i:i + 1], bS[i % 2][:], AX_X, ALU.max, negate=True).then_inc(d_max, 1)
                        if ph == FACTOR_FROM:
                            build()
                        gated(v_at(b, i), Va[:, i, :], gh[:, 0, :, :], b * TB + i, True, parts_of(ph))
                        if ph == FACTORED:
                            finish_factor()
                    if b < NB - 1:
                        project(b + 1)
                    dve.wait_ge(p_quart, FIRST + h * QUARTS + v_at(b, TB - 1) + 1)
                    dve.wait_ge(d_gate, FIRST + h * (GH * ND) + GH * DVE_AT[v_at(b, TB - 1) + 1])
                    v.tensor_tensor(Va[:], Va[:], Vb[:], ALU.add).then_inc(d_V, 1)
                    dve.wait_ge(a_exp, h * NB * TB + (b + 1) * TB)
                    v.reciprocal(rinv[:], rsum[:, b % 2, :]).then_inc(d_rinv, 1)
                    if b >= 2:
                        dve.wait_ge(a_cp, FIRST + h * (GH * NA) + GH * (act_at(o_at(b - 2, TB - 1), 1) + 1))
                    dve.wait_ge(d_rinv, h * NB + b + 1)
                    v.tensor_tensor(goh[:, b % 2, :, :], gh[:, 1, b * TB:(b + 1) * TB, :],
                                    rinv[:].rearrange("p (k a) -> p k a", a=1).broadcast_to([P, TB, NE]), ALU.mult).then_inc(d_goh, 1)
                    for j in range(TB):
                        n = h * NB * TB + b * TB + j
                        ph = b * 2 * TB + TB + j
                        between = parts_of(ph)
                        dve.wait_ge(a_PTh, n + 1)
                        v.tensor_tensor(pTl[:, j % 2, :], bPT[:], pTh[:, j % 2, :].bitcast(F32), ALU.subtract).then_inc(d_PTl, 1)
                        if j == 0:
                            dve.wait_ge(a_Vh, h * NB + b + 1)
                            v.tensor_tensor(Vl[:], Va[:].rearrange("p b d -> p (b d)"), Vh[:].bitcast(F32), ALU.subtract).then_inc(d_Vl, 1)
                        if b:
                            output(b - 1, j, between)
                        else:
                            for part in between:
                                eliminate(*part)
                        if ph == FACTORED:
                            finish_factor()
                    dve.wait_ge(a_C, h * NB + b + 1)
                    v.tensor_tensor(cl[:], bC[:], ch[:].bitcast(F32), ALU.subtract).then_inc(d_C, 1)
                for j in range(TB):
                    output(NB - 1, j, [])
                for f, change in enumerate((bU, bC)):
                    dve.wait_ge(c_up, h * 2 + f + 1)
                    v.tensor_tensor(A[:, f, :, :].rearrange("p b d -> p (b d)"), A[:, f, :, :].rearrange("p b d -> p (b d)"), change[:],
                                    ALU.subtract).then_inc(c_A, 1)

            dve.wait_ge(p_acc, FIRST + NH * NB * TB)
            dve.wait_ge(d_gate, FIRST + NH * GH * ND)
            for b in range(NB):
                for i in range(TB):
                    dve.wait_ge(f_p, b * TB + i + 1)
                    v.tensor_tensor(pT[:, i % 2, 0:P], bS[i % 2][:, 0:P], causal[:], ALU.mult).then_inc(f_diag, 1)
                k = slice(b * TB, (b + 1) * TB)
                link(v.tensor_tensor(xn[:, k, :], acc[:, k, :], acc2[:, k, :], ALU.add))
                link(v.tensor_tensor(xn[:, k, :], xn[:, k, :], x_sb[:, k, :], ALU.add))
                link(v.tensor_tensor(xn[:, k, :], xn[:, k, :], bo_b[:].rearrange("p (a d) -> p a d", a=1).broadcast_to([P, TB, P]), ALU.add))
                dve.wait_ge(f_y, b + 1)
                q = v.tensor_tensor(xn[:, k, :].rearrange("p k d -> p (k d)"), xn[:, k, :].rearrange("p k d -> p (k d)"), bPT[:], ALU.add)
                q.then_inc(f_take, 1)
                dve.wait_ge(f_take, b + 1)
                q = v.tensor_scalar(x_sb[:, k, :], xn[:, k, :], 1.0, None, ALU.mult)
                q.then_inc(f_res, 1)


_INS = ['L0_attn_x', 'L0_attn_Wq', 'L0_attn_bq', 'L0_attn_Wk', 'L0_attn_bk', 'L0_attn_Wv', 'L0_attn_bv', 'L0_attn_Wo', 'L0_attn_bo',
        'L0_ffn_q_w', 'L0_ffn_k_w', 'L0_ffn_v_w', 'L0_ffn_o_w', 'L0_ffn_sel_v_w', 'L0_ffn_sel_o_w', 'L0_ffn_route_scale']


def kernel(**inputs):
    import numpy as np
    import concourse.bacc as bacc
    from concourse.bass_utils import run_bass_kernel_spmd

    nc = bacc.Bacc("TRN2", target_bir_lowering=False, num_devices=1)
    arrays, args = {}, []
    for name in _INS:
        a = np.ascontiguousarray(inputs[name])
        arrays[name] = a
        args.append(nc.dram_tensor(name, a.shape, mybir.dt.from_np(a.dtype), kind="ExternalInput").ap())
    shape = inputs['L0_attn_x'].shape
    out = nc.dram_tensor("out", shape, F32, kind="ExternalOutput").ap()
    block_kernel(nc, *args, out)
    r = run_bass_kernel_spmd(nc, [arrays], core_ids=[0])
    return r.results[0]["out"]
```

```python
from contextlib import ExitStack

import concourse.bass as bass
from concourse import mybir

ALU = mybir.AluOpType
ACT = mybir.ActivationFunctionType
F32 = mybir.dt.float32
F32R = mybir.dt.float32r
AX_X = mybir.AxisListType.X

P = 128
LN_EPS = 1e-5
NORM_EPS = 1e-6
TINY = 1e-30
MOST = 3e38
BEYOND = 3.2e38
CHUNK = 32
FIRST = 40

ELIMINATION_STEPS = (1, 1, 1, 1, 2, 2, 2, 2)


class Plan:

    def __init__(self, on_dve, before):
        self.on_dve, self.before = on_dve, before
        self.dve = sum(on_dve)
        self.act = 2 * len(on_dve) - self.dve
        self.sums = 2 * len(on_dve) - self.dve

    def dve_at(self, n):
        return sum(self.on_dve[:n])

    def act_at(self, n, g):
        return 2 * n + g - self.dve_at(n) - (1 if g and self.on_dve[n] else 0)

    def dve_has(self, m):
        return self.on_dve[m] if m >= 0 else self.before[m]

    def dve_upto(self, m):
        return self.dve_at(m + 1) if m >= 0 else -sum(self.before[m + 1:] if m < -1 else ())

    def act_upto(self, m, g):
        if m >= 0:
            return self.act_at(m, g) + 1
        last = Plan(self.before, self.before)
        return last.act_at(m + len(self.before), g) + 1 - last.act

    def taken(self, k):
        if k < 0:
            last = Plan(self.before, self.before)
            return last.taken(k + last.act) - last.sums
        at = 0
        for n, dve_has in enumerate(self.on_dve):
            at += 1 if dve_has else 2
            if k < at:
                return self.act_at(n, 0) + 1


def block_kernel(nc, x, Wq, bq, Wk, bk, Wv, bv, Wo, bo, q_w, k_w, v_w, o_w, sel_v_w, sel_o_w, route_scale, out):
    NB, SEQ, D = x.shape
    NH = q_w.shape[0] // P
    NE = v_w.shape[0] // NH
    TB = SEQ // P
    NT = NB * TB
    GH = NE // 2
    GATES = 2 * NH * NE
    SCALE = float(P) ** -0.5
    assert D == P and NB * CHUNK == P and GATES == P and GH * P == 512 and SEQ == 512

    with ExitStack() as ctx:
        def sb(name, shape, dt=F32):
            return ctx.enter_context(nc.sbuf_tensor(name, shape, dt))

        def bank(name):
            return ctx.enter_context(nc.psum_tensor(name, [P, 512], F32))

        def sem(name):
            return ctx.enter_context(nc.semaphore(name))

        x_sb = sb("x_sb", [P, NT, D])
        xn = sb("xn", [P, NT, D])
        xh = sb("xh", [P, NT * P], F32R)
        xl = sb("xl", [P, NT * P], F32R)
        stats = sb("stats", [P, NT, 6])
        mv = sb("mv", [P, NT, 2])
        rstd = sb("rstd", [P, NT])
        small_a = sb("small_a", [P, NT])
        small_b = sb("small_b", [P, NT])
        ident = sb("ident", [P, P])
        w4 = sb("w4", [P, 4, D])
        w3h = sb("w3h", [P, 3 * P], F32R)
        w3l = sb("w3l", [P, 3 * P], F32R)
        woT = sb("woT", [P, P])
        sel = sb("sel", [P, D])
        selh = sb("selh", [P, P], F32R)
        sell = sb("sell", [P, P], F32R)
        bias3 = sb("bias3", [P, 3, P])
        bv_c = sb("bv_c", [P, 1])
        woTb = sb("woTb", [P, P])
        ones = sb("ones", [P, P])
        bo_b = sb("bo_b", [P, P])
        rs_b = sb("rs_b", [P, 1])
        qkv = sb("qkv", [P, NT, 3, P])
        kq = sb("kq", [P, NT])
        kk = sb("kk", [P, NT])
        kn = sb("kn", [P, NT])
        uT = sb("uT", [P, NB, SEQ])
        qT = sb("qT", [P, NB, SEQ])
        prob = sb("prob", [P, NT, GATES])
        pick = sb("pick", [P, NT, GATES])
        tmpg = sb("tmpg", [P, NT, GATES])
        gate = sb("gate", [P, NT, GATES])
        rank = sb("rank", [P, NE])
        NG = NT * 2 * NH
        top1 = sb("top1", [P, NG])
        top2 = sb("top2", [P, NG])
        topr = sb("topr", [P, NG])
        A = sb("A", [P, 2, NB, P])
        uTc = sb("uTc", [P, 2, NB, CHUNK])
        AuT = sb("AuT", [P, 2, NB, CHUNK])
        uA = sb("uA", [P, 2, P])
        M = sb("M", [P, 2, 2 * CHUNK])
        eye32 = sb("eye32", [P, CHUNK])
        nmask = sb("nmask", [P, CHUNK])
        nlow = sb("nlow", [P, P])
        row = sb("row", [P, 2, CHUNK + 1])
        rp = sb("rp", [P, 2])
        cf = sb("cf", [P, 2])
        Dv = sb("Dv", [P, 2])
        rDf = sb("rDf", [P, 2])
        scr32 = sb("scr32", [P, CHUNK])
        Rbd = sb("Rbd", [P, 2, P])
        Wc = sb("Wc", [P, 2, P])
        Zc = sb("Zc", [P, 2, P])
        Zbd = sb("Zbd", [P, 2, NB, P])
        B0 = Zbd[:, 0, :, :]
        Y0 = Zbd[:, 1, :, :]
        own = sb("own", [P, NB])
        zT = sb("zT", [P, NB, SEQ])
        causal = sb("causal", [P, P])
        qk_raw = sb("qk_raw", [P, 2, P])
        Ah = sb("Ah", [P, P], F32R)
        Al = sb("Al", [P, P], F32R)
        vo_raw = sb("vo_raw", [P, 2, NE * P])
        vo_h = sb("vo_h", [P, 2, NE * P], F32R)
        vo_l = sb("vo_l", [P, 2, NE * P], F32R)
        Th = sb("Th", [P, 512], F32R)
        Tl = sb("Tl", [P, 512], F32R)
        gh = sb("gh", [P, 2, NT, NE])
        goh = sb("goh", [P, 2, TB, NE])
        nmax = sb("nmax", [P, 2, TB])
        rsum = sb("rsum", [P, 2, TB])
        rinv = sb("rinv", [P, TB])
        prb = tmpg[:].rearrange("p a b -> p (a b)").rearrange("p (k n) -> p k n", k=TB)
        pTs = sb("pTs", [P, 2, 512])
        Va = sb("Va", [P, TB, P])
        Vb = sb("Vb", [P, TB, P])
        Vs = sb("Vs", [P, TB, P])
        ch = sb("ch", [P, 512], F32R)
        cl = sb("cl", [P, 512], F32R)
        tmp = xn[:].rearrange("p (n e) d -> p n e d", e=GH)
        half = sb("half", [P, 2, P])
        quart = sb("quart", [P, P])
        both = sb("both", [P, GH, P])
        acc, acc2 = x_sb, qkv[:, :, 1, :]

        id2 = sb("id2", [P, P])
        unused = sb("unused", [P, 2])
        id2_r = sb("id2_r", [P, P], F32R)
        ident_r = sb("ident_r", [P, P], F32R)
        bS = [bank("bS0"), bank("bS1")]
        bPT = bank("bPT")
        bC = bank("bC")
        bY = [bank("bY0"), bank("bY1")]
        bG = bank("bG")
        bU = bank("bU")
        lg_banks = [bY[0], bY[1], bC, bPT]
        newton_banks = [(bPT, bC), (bY[0], bY[1])]
        first_Y = [bY[0], bU]

        def sems(names):
            return [sem(n) for n in names.split()]

        ld_x = [sem(f"ld_x{b}") for b in range(NB)]
        ld_bv, ld_w, ld_b, ld_qk, ld_v, ld_o, stored, zero_ok, ident_ok, pro_p = sems(
            "ld_bv ld_w ld_b ld_qk ld_v ld_o stored zero_ok ident_ok pro_p")
        var_ok, root_ok, xn_ok, kk_ok, kroot_ok, unit_ok, link_ok, acc_ok = sems(
            "var_ok root_ok xn_ok kk_ok kroot_ok unit_ok link_ok acc_ok")
        xT_mm, xh_ok, xl_ok, wT_mm, wh_ok, wl_ok, qkv_mm, qkv_ok, lg_mm = sems(
            "xT_mm xh_ok xl_ok wT_mm wh_ok wl_ok qkv_mm qkv_ok lg_mm")
        lg_ok, ut_mm, ut_ok, c_uT, c_au, c_uA, c_auT, c_auE, c_g, c_fac, elim_ok = sems(
            "lg_ok ut_mm ut_ok c_uT c_au c_uA c_auT c_auE c_g c_fac elim_ok")
        n_mm, n_B, n_ev, kn_ok, value_ok, c_Zbd, c_W, c_WE, c_z, c_zE, c_up, c_A, s_A, s_T, s_S = sems(
            "n_mm n_B n_ev kn_ok value_ok c_Zbd c_W c_WE c_z c_zE c_up c_A s_A s_T s_S")
        s_Y0, s_Y1, s_PT, s_PV, a_A, d_A, a_wv, p_wv, a_wo, p_wo, a_T = sems(
            "s_Y0 s_Y1 s_PT s_PV a_A d_A a_wv p_wv a_wo p_wo a_T")
        d_T, d_max, a_exp, d_gate, d_gh, d_V, a_cp = sems(
            "d_T d_max a_exp d_gate d_gh d_V a_cp")
        p_half, p_quart, p_acc, a_PT, a_C, d_C, d_rinv, d_goh, nil_ok = sems(
            "p_half p_quart p_acc a_PT a_C d_C d_rinv d_goh nil_ok")
        f_p, f_diag, f_rest, f_o, f_sum, f_res = sems("f_p f_diag f_rest f_o f_sum f_res")
        block = ctx.enter_context(nc.Block())

        x_v = x.rearrange("b (k p) d -> p (b k) d", p=P)
        out_v = out.rearrange("b (k p) d -> p (b k) d", p=P)
        qw_v = q_w.rearrange("(h p) d -> p h d", p=P)
        kw_v = k_w.rearrange("(h p) d -> p h d", p=P)
        vw_v = v_w.rearrange("(h e) d p -> d h e p", e=NE)
        ow_v = o_w.rearrange("(h e) p d -> p h e d", e=NE)

        def v_at(b, i):
            return 2 * TB * b + i

        def o_at(b, j):
            return 2 * TB * b + TB + j

        NEWTON = 11
        WORST = SEQ // 2 + 1
        ALPHA = 2.0 / (WORST + 1)

        ON_DVE = sum([[True] * TB + [b == NB - 1] * TB for b in range(NB)], [])
        ON_DVE_END = [True] * TB
        STEPS = len(ON_DVE)
        head = Plan(ON_DVE, ON_DVE)
        end = Plan(ON_DVE_END, ON_DVE)

        PHASES = 2 * NB * TB
        BUILD_AT = TB - 1
        PARTS_OF, step, count = [], 0, 2
        for ph in range(PHASES):
            parts = []
            for _ in range(0 if ph <= BUILD_AT else ELIMINATION_STEPS[ph % (2 * TB)]):
                if step < CHUNK - 1:
                    n = 8 if ph % (2 * TB) >= TB else 5
                    parts += [(step, n, part, count) for part in range(n)]
                    step, count = step + 1, count + n
            PARTS_OF.append(parts)
        ELIMINATED = count
        FACTORED = max(ph for ph in range(PHASES) if PARTS_OF[ph])
        UPDATE_AT = 2 * TB * (NB - 1)
        assert step == CHUNK - 1 and NH * CHUNK == SEQ // 2 and FACTORED < UPDATE_AT

        pT = [prb, gate[:].rearrange("p a b -> p (a b)").rearrange("p (k n) -> p k n", k=TB)]
        zq_banks = [bS[0], bS[1], bG]

        def rest(n):
            return n // TB * (TB - 1) + min(n % TB + 1, TB - 1)

        def second_Y(side, n):
            return bPT if side == 0 and n % 2 == 0 else bY[1]

        @block.sync
        def _(sp):
            for b in range(NB):
                sp.dma_start(x_sb[:, b * TB:(b + 1) * TB, :], x_v[:, b * TB:(b + 1) * TB, :]).then_inc(ld_x[b], 16)
            for n, w in enumerate((Wq, Wk, Wv, Wo)):
                sp.dma_start(w4[:, n, :], w).then_inc(ld_w, 16)
            sp.dma_start(sel[0:P // 2, :], sel_v_w).then_inc(ld_w, 16)
            sp.dma_start(sel[P // 2:P, :], sel_o_w).then_inc(ld_w, 16)
            sp.dma_start(bv_c[:], bv.rearrange("(d a) -> d a", a=1)).then_inc(ld_bv, 16)
            for n, w in enumerate((bq, bk)):
                sp.dma_start(bias3[:, n, :], w.rearrange("(a d) -> a d", a=1).broadcast_to([P, P])).then_inc(ld_b, 16)
            sp.dma_start(bo_b[:], bo.rearrange("(a d) -> a d", a=1).broadcast_to([P, P])).then_inc(ld_b, 16)
            sp.dma_start(rs_b[:], route_scale.rearrange("(a d) -> a d", a=1).broadcast_to([P, 1])).then_inc(ld_b, 16)

            def load_qk(h):
                sp.dma_start(qk_raw[:, 0, :], qw_v[:, bass.ds(h, 1), :].rearrange("p a d -> p (a d)")).then_inc(ld_qk, 16)
                sp.dma_start(qk_raw[:, 1, :], kw_v[:, bass.ds(h, 1), :].rearrange("p a d -> p (a d)")).then_inc(ld_qk, 16)

            def load_v(h):
                sp.dma_start(vo_raw[:, 0, :].rearrange("p (e d) -> p e d", e=NE),
                             vw_v[:, bass.ds(h, 1), :, :].rearrange("p a e d -> p (a e) d")).then_inc(ld_v, 16)

            def load_o(h):
                sp.dma_start(vo_raw[:, 1, :].rearrange("p (e d) -> p e d", e=NE),
                             ow_v[:, bass.ds(h, 1), :, :].rearrange("p a e d -> p (a e) d")).then_inc(ld_o, 16)

            load_qk(0)
            load_v(0)
            load_o(0)
            sp.wait_ge(s_A, 1)
            load_qk(1)
            sp.wait_ge(a_wv, 1)
            sp.wait_ge(p_wv, 1)
            load_v(1)
            with sp.Fori(0, NH - 2) as h:
                sp.wait_ge(a_wo, FIRST + h + 1)
                sp.wait_ge(p_wo, FIRST + h + 1)
                load_o(h + 1)
                sp.wait_ge(s_A, h + 2)
                load_qk(h + 2)
                sp.wait_ge(a_wv, h + 2)
                sp.wait_ge(p_wv, h + 2)
                load_v(h + 2)
            sp.wait_ge(a_wo, FIRST + NH - 1)
            sp.wait_ge(p_wo, FIRST + NH - 1)
            load_o(NH - 1)
            sp.wait_ge(s_A, NH)
            load_qk(NH - 1)
            sp.wait_ge(a_wv, NH)
            sp.wait_ge(p_wv, NH)
            load_v(NH - 1)
            for b in range(NB):
                sp.wait_ge(f_res, b + 1)
                sp.dma_start(out_v[:, b * TB:(b + 1) * TB, :], x_sb[:, b * TB:(b + 1) * TB, :]).then_inc(stored, 16)
            sp.wait_ge(stored, 16 * NB)

        @block.gpsimd
        def _(pool):
            for started in (p_quart, p_acc, p_half, p_wo):
                pool.sem_inc(started, FIRST)
            g = nc.gpsimd
            g.memset(ident[:], 0.0).then_inc(pro_p, 1)
            g.memset(nlow[:], -1.0).then_inc(pro_p, 1)
            g.memset(causal[:], 1.0).then_inc(pro_p, 1)
            g.memset(id2[:], 0.0).then_inc(pro_p, 1)
            g.memset(ones[:], 1.0).then_inc(pro_p, 1)
            pool.wait_ge(pro_p, 5)
            g.affine_select(out=ident[:], in_=ident[:], compare_op=ALU.not_equal, fill=1.0, base=0,
                            pattern=[[-1, P]], channel_multiplier=1).then_inc(ident_ok, 1)
            g.affine_select(out=nlow[:], in_=nlow[:], compare_op=ALU.is_gt, fill=0.0, base=0,
                            pattern=[[-1, P]], channel_multiplier=1).then_inc(ident_ok, 1)
            g.affine_select(out=causal[:], in_=causal[:], compare_op=ALU.is_ge, fill=0.0, base=0,
                            pattern=[[1, P]], channel_multiplier=-1).then_inc(ident_ok, 1)
            g.affine_select(out=id2[:], in_=id2[:], compare_op=ALU.not_equal, fill=2.0, base=0,
                            pattern=[[-1, P]], channel_multiplier=1).then_inc(ident_ok, 1)
            pool.wait_ge(ident_ok, 4)
            each = ident[:].rearrange("p (a d) -> p a d", a=1).broadcast_to([P, NB, P])
            g.tensor_scalar(A[:, 0, :, :], each, 1.0, None, ALU.mult).then_inc(zero_ok, 1)
            g.tensor_scalar(A[:, 1, :, :], each, ALPHA, None, ALU.mult).then_inc(zero_ok, 1)
            for e in range(NE):
                g.memset(rank[:, e:e + 1], float(NE - e)).then_inc(zero_ok, 1)
            g.memset(Rbd[:], 0.0).then_inc(zero_ok, 1)
            for nil in (ch[:], cl[:], vo_h[:, 1, :], vo_l[:, 1, :], goh[:, 1, :, :]):
                g.memset(nil.bitcast(F32), 0.0).then_inc(nil_ok, 1)

            def split(side, ready, done):
                g.tensor_tensor(vo_l[:, side, :], vo_raw[:, side, :], vo_h[:, side, :].bitcast(F32), ALU.subtract).then_inc(done, 1)

            pool.wait_ge(xn_ok, NB)
            pool.wait_ge(ld_b, 64)
            g.tensor_tensor(acc[:], x_sb[:], bo_b[:].rearrange("p (a d) -> p a d", a=1).broadcast_to([P, NT, P]), ALU.add).then_inc(acc_ok, 1)
            pool.wait_ge(kk_ok, 2)
            for k in range(NT):
                q = g.tensor_scalar(qkv[:, k, 2, :], qkv[:, k, 2, :], kq[:, k:k + 1], None, ALU.mult)
            q.then_inc(value_ok, 1)
            pool.wait_ge(n_B, NB)
            g.memset(acc2[:], 0.0).then_inc(acc_ok, 1)
            pool.wait_ge(a_wv, 1)
            split(0, a_wv, p_wv)
            pool.wait_ge(acc_ok, 2)

            def halve(plan, turn, n, in_):
                last = plan.dve_at(n)
                pool.wait_ge(p_quart, FIRST + turn * STEPS + n)
                g.tensor_tensor(half[:], in_[:, 0:2, :], in_[:, 2:4, :], ALU.add).then_inc(p_half, 1)
                pool.wait_ge(p_half, FIRST + turn * head.sums + plan.act_at(n, 1) + 1)

            def value(h, b, i):
                n = v_at(b, i)
                k = head.act_at(n, 1)
                pool.wait_ge(a_cp, FIRST + h * (GH * head.act) + GH * (k + 1))
                halve(head, h, n, tmp[:, k % 4, :, :])
                g.tensor_tensor(Vb[:, i, :], half[:, 0, :], half[:, 1, :], ALU.add).then_inc(p_quart, 1)

            def output(plan, h, n, o, b, j):
                k = plan.act_at(n, 1)
                pool.wait_ge(a_cp, FIRST + h * (GH * head.act) + GH * (k + 1))
                if plan.on_dve[n]:
                    halve(plan, h, n, tmp[:, k % 4, :, :])
                else:
                    pool.wait_ge(p_half, FIRST + h * head.sums + k - 1)
                    g.tensor_tensor(both[:], tmp[:, (k - 1) % 4, :, :], tmp[:, k % 4, :, :], ALU.add).then_inc(p_half, 1)
                    pool.wait_ge(p_half, FIRST + h * head.sums + k)
                    halve(plan, h, n, both[:])
                pool.wait_ge(p_acc, FIRST + h * (NB * TB) + o)
                g.tensor_tensor(quart[:], half[:, 0, :], half[:, 1, :], ALU.add).then_inc(p_quart, 1)
                pool.wait_ge(p_quart, FIRST + h * STEPS + n + 1)
                m = b * TB + j
                g.tensor_tensor(acc2[:, m, :], acc2[:, m, :], quart[:], ALU.add).then_inc(p_acc, 1)

            with pool.Fori(0, NH) as h:
                for b in range(NB):
                    pool.wait_ge(d_V, FIRST + h * NB + b)
                    for i in range(TB):
                        value(h, b, i)
                        if b == 1 and i == 0:
                            pool.wait_ge(a_wo, FIRST + h + 1)
                            split(1, a_wo, p_wo)
                        if b == NB - 1 and i == 1:
                            for f in range(2):
                                pool.wait_ge(c_WE, h * 3 + 2 + f)
                                g.tensor_tensor(Zbd[:, f, :, :], Zc[:, f, :].rearrange("p (a d) -> p a d", a=1).broadcast_to([P, NB, P]),
                                                own[:].rearrange("p (b a) -> p b a", a=1).broadcast_to([P, NB, P]), ALU.mult).then_inc(c_Zbd, 1)
                    for j in range(TB):
                        output(head, h, o_at(b, j), b * TB + j, (b - 1) % NB, j)
                        if b == NB - 1 and j == 0:
                            pool.wait_ge(a_wv, h + 2)
                            split(0, a_wv, p_wv)
            for j in range(TB):
                output(end, NH, j, j, NB - 1, j)

        @block.tensor
        def _(pe):
            for started in (c_g, s_Y0, s_Y1, s_PV):
                pe.sem_inc(started, FIRST)
            t = nc.tensor

            def mm3(out_, ah, al, bh, bl, start=True, stop=True):
                t.matmul(out_, ah, bh, start=start, stop=False)
                t.matmul(out_, ah, bl, start=False, stop=False)
                return t.matmul(out_, al, bh, start=False, stop=stop)

            def project(b, turn):
                pe.wait_ge(a_A, turn + 1)
                pe.wait_ge(d_A, turn + 1)
                c = slice(b * 512, (b + 1) * 512)
                mm3(bS[0][:], Ah[:], Al[:], xh[:, c], xl[:, c]).then_inc(s_T, 1)

            pe.wait_ge(ident_ok, 1)
            pe.wait_ge(ld_w, 96)
            for n in (3, 0, 1):
                t.transpose(bY[0][:, n * P:(n + 1) * P], w4[:, n, :], ident[:]).then_inc(wT_mm, 1)
            t.transpose(bY[1][:, 0:P], sel[:], ident[:]).then_inc(wT_mm, 1)
            pe.wait_ge(wh_ok, 2)
            t.matmul(bG[:, 0:P], w4[:, 2, :], woT[:], start=True, stop=True)
            t.matmul(bG[:, P:2 * P], ones[:], woTb[:], start=True, stop=True).then_inc(wT_mm, 1)
            for b in range(NB):
                pe.wait_ge(xn_ok, b + 1)
                if b >= 2:
                    pe.wait_ge(xl_ok, b - 1)
                for i in range(TB):
                    q = t.transpose(bS[b % 2][:, i * P:(i + 1) * P], xn[:, b * TB + i, :], ident[:])
                q.then_inc(xT_mm, 1)
            pe.wait_ge(wh_ok, 6)
            pe.wait_ge(wl_ok, 3)
            for k in range(NT):
                pe.wait_ge(xh_ok, k // TB + 1)
                pe.wait_ge(xl_ok, k // TB + 1)
                c = slice(k * P, (k + 1) * P)
                q = mm3(lg_banks[k // TB][:, k % TB * P:(k % TB + 1) * P], xh[:, c], xl[:, c], selh[:], sell[:])
                if k % TB == TB - 1:
                    q.then_inc(lg_mm, 1)
                if k >= 2:
                    pe.wait_ge(qkv_ok, k - 1)
                mm3((bG, bU)[k % 2][:, 0:3 * P], xh[:, c], xl[:, c], w3h[:], w3l[:]).then_inc(qkv_mm, 1)
            for n in range(2 * NB):
                b = n % NB
                if n < NB:
                    pe.wait_ge(qkv_ok, NT)
                else:
                    pe.wait_ge(unit_ok, b + 1)
                if n >= 2:
                    pe.wait_ge(ut_ok, n - 1)
                for i in range(TB):
                    q = t.transpose(bS[n % 2][:, i * P:(i + 1) * P], qkv[:, b * TB + i, 0 if n < NB else 1, :], ident[:])
                q.then_inc(ut_mm, 1)
                if n == 0:
                    pe.wait_ge(ld_qk, 32)
                    t.matmul(bU[:, 0:P], qk_raw[:, 0, :], qk_raw[:, 1, :], start=True, stop=True).then_inc(s_A, 1)
                if n >= NB:
                    gram = newton_banks[b // 2][1][:, b % 2 * P:(b % 2 + 1) * P]
                    pe.wait_ge(lg_ok, NB)
                    t.matmul(gram, ident[:], ident[:], start=True, stop=False)
                    for k in range(TB // 2):
                        u = qkv[:, b * TB + k, 1, :]
                        q = t.matmul(gram, u, u, start=False, stop=(k == TB // 2 - 1))
                    q.then_inc(n_B, 1)
            pe.wait_ge(ut_ok, 2 * NB)
            project(0, 0)

            pe.wait_ge(zero_ok, NE + 3)
            for n in range(NEWTON):
                for c in range(2):
                    pe.wait_ge(n_ev, 4 * n + c + 1)
                    for b in (2 * c, 2 * c + 1):
                        into = newton_banks[c][0][:, b % 2 * P:(b % 2 + 1) * P]
                        t.matmul(into, id2_r[:], ident_r[:], start=True, stop=False)
                        q = t.matmul(into, B0[:, b, :], A[:, 1, b, :], start=False, stop=True)
                    q.then_inc(n_mm, 1)
                for c in range(2):
                    pe.wait_ge(n_ev, 4 * n + c + 3)
                    for b in (2 * c, 2 * c + 1):
                        q = t.matmul(newton_banks[c][1][:, b % 2 * P:(b % 2 + 1) * P], A[:, 1, b, :], Y0[:, b, :], start=True, stop=True)
                    q.then_inc(n_mm, 1)

            def expert(plan, turn, side, n, lh, ll):
                for g, ready in enumerate((s_Y0, s_Y1)):
                    e = slice(g * 512, (g + 1) * 512)
                    m = n - 2 if g == 0 or side == 0 else n - 1
                    if g == 0 and plan.dve_has(m):
                        pe.wait_ge(d_gate, FIRST + turn * (GH * head.dve) + GH * plan.dve_upto(m))
                    else:
                        pe.wait_ge(a_cp, FIRST + turn * (GH * head.act) + GH * plan.act_upto(m, g))
                    into = first_Y[n % 2] if g == 0 else second_Y(side, n)
                    mm3(into[:], lh, ll, vo_h[:, side, e], vo_l[:, side, e]).then_inc(ready, 1)

            def output(plan, h, n, j, batches):
                c = slice(j * P, (j + 1) * P)
                if j == 0:
                    pe.wait_ge(a_C, FIRST + batches)
                    pe.wait_ge(d_C, FIRST + batches)
                expert(plan, h, 1, n, ch[:, c], cl[:, c])

            def rec_au():
                pe.wait_ge(c_uT, h + 1)
                pe.wait_ge(c_zE, FIRST + h * 2)
                pe.wait_ge(c_A, FIRST + h * 2)
                for f in range(2):
                    for b in range(NB):
                        q = t.matmul(bG[b * CHUNK:(b + 1) * CHUNK, 2 * P + f * P:3 * P + f * P], uTc[:, f, b, :], A[:, f, b, :],
                                     start=True, stop=True)
                q.then_inc(c_au, 1)

            def rec_transpose():
                pe.wait_ge(c_uA, h + 1)
                for f in range(2):
                    q = t.transpose(bG[:, f * P:(f + 1) * P], uA[:, f, :], ident[:])
                q.then_inc(c_auT, 1)

            def rec_gram():
                pe.wait_ge(c_auE, h + 1)
                for f in range(2):
                    for b in range(NB):
                        q = t.matmul(bG[b * CHUNK:(b + 1) * CHUNK, f * CHUNK:(f + 1) * CHUNK], uTc[:, f, b, :], AuT[:, f, b, :],
                                     start=True, stop=True)
                q.then_inc(c_g, 1)

            def rec_w():
                pe.wait_ge(c_fac, h + 1)
                for f in range(2):
                    q = t.matmul(bG[:, 2 * P + f * P:3 * P + f * P], Rbd[:, f, :], uA[:, f, :], start=True, stop=True)
                q.then_inc(c_W, 1)

            def rec_update():
                pe.wait_ge(c_Zbd, h * 2 + 2)
                pe.wait_ge(a_A, h + 2)
                pe.wait_ge(d_A, h + 2)
                pe.wait_ge(a_cp, FIRST + h * (GH * head.act) + GH * head.act_upto(v_at(NB - 1, TB - 2), 1))
                for f, into in enumerate((bPT, bC)):
                    t.matmul(into[:], Wc[:, f, :], Zbd[:, f, :, :].rearrange("p b d -> p (b d)"), start=True, stop=True).then_inc(c_up, 1)
                for f in range(2):
                    q = t.transpose(bG[:, f * P:(f + 1) * P], Zc[:, f, :], ident[:])
                q.then_inc(c_z, 1)

            pe.wait_ge(n_ev, 4 * NEWTON + 2)
            pe.wait_ge(nil_ok, 5)
            with pe.Fori(0, NH) as h:
                pe.wait_ge(a_wv, h + 1)
                pe.wait_ge(p_wv, h + 1)
                for b in range(NB):

                    def scores(i, b=b):
                        c = slice(i * P, (i + 1) * P)
                        kc = slice(b * 512, (b + 1) * 512)
                        if i == 0:
                            pe.wait_ge(a_T, h * NB + b + 1)
                            pe.wait_ge(d_T, h * NB + b + 1)
                        if i >= 2:
                            pe.wait_ge(a_exp, h * NB * TB + b * TB + i - 1)
                        mm3(bS[i % 2][:], Th[:, c], Tl[:, c], xh[:, kc], xl[:, kc]).then_inc(s_S, 1)

                    if b == 0:
                        scores(0)
                    for i in range(TB):
                        if i < TB - 1:
                            scores(i + 1)
                        if i == TB - 1:
                            pe.wait_ge(a_exp, h * NB * TB + b * TB + i)
                            project((b + 1) % NB, h + (b + 1) // NB)
                        xc = slice((b * TB + i) * P, (b * TB + i + 1) * P)
                        if i == 0:
                            pe.wait_ge(a_PT, FIRST + h * (NB * TB) + b * TB)
                        expert(head, h, 0, v_at(b, i), xh[:, xc], xl[:, xc])
                        if b == 0 and i == 0:
                            rec_au()
                        if b == 0 and i == 1:
                            rec_transpose()
                        if b == 0 and i == 2:
                            rec_gram()
                        if b == NB - 1 and i == 0:
                            rec_w()
                        if b == NB - 1 and i == 1:
                            pe.wait_ge(ld_qk, h * 32 + 64)
                            pe.wait_ge(a_C, FIRST + h * NB + b)
                            pe.wait_ge(d_C, FIRST + h * NB + b)
                            t.matmul(bC[:, 0:P], qk_raw[:, 0, :], qk_raw[:, 1, :], start=True, stop=True).then_inc(s_A, 1)
                        if b == NB - 1 and i == TB - 1:
                            rec_update()
                    pe.wait_ge(a_exp, h * NB * TB + (b + 1) * TB)
                    if b == 1:
                        pe.wait_ge(a_wo, FIRST + h + 1)
                        pe.wait_ge(p_wo, FIRST + h + 1)

                    def weigh(j):
                        n = h * NB * TB + b * TB + j
                        if j == 0:
                            pe.wait_ge(d_V, FIRST + h * NB + b + 1)
                            pe.wait_ge(d_C, FIRST + h * NB + b)
                            pe.wait_ge(a_C, FIRST + h * NB + b)
                            if b == NB - 1:
                                pe.wait_ge(c_A, FIRST + h * 2 + 2)
                        pe.wait_ge(a_PT, FIRST + n + 1)
                        t.matmul(bC[:], Vs[:, j, :], pTs[:, j % 2, :], start=(j == 0), stop=(j == TB - 1)).then_inc(s_PV, 1)

                    for j in range(TB):
                        n = h * NB * TB + b * TB + j
                        pe.wait_ge(a_PT, FIRST + n)
                        if j == 0:
                            pe.wait_ge(a_cp, FIRST + h * (GH * head.act) + GH * head.act_upto(v_at(b, TB - 2), 1))
                        if b == NB - 1 and j == 0:
                            pe.wait_ge(c_A, FIRST + h * 2 + 1)
                        for i in range(TB):
                            q = t.transpose(bPT[:, i * P:(i + 1) * P], prb[:, i, j * P:(j + 1) * P], ident[:])
                        q.then_inc(s_PT, 1)
                        output(head, h, o_at(b, j), j, h * NB + b)
                        if j:
                            weigh(j - 1)
                    if b < NB - 1:
                        scores(0, b + 1)
                    weigh(TB - 1)

            pe.wait_ge(value_ok, 1)
            pe.wait_ge(c_zE, FIRST + NH * 2)
            pe.wait_ge(a_T, NH * NB + 1)
            pe.wait_ge(d_T, NH * NB + 1)
            pe.wait_ge(a_PT, FIRST + NH * NB * TB)

            def weigh(b):
                if b >= 2:
                    pe.wait_ge(f_res, b - 1)
                for j in range(TB):
                    pe.wait_ge(f_diag, b * TB + j + 1)
                    if j:
                        pe.wait_ge(f_rest, rest(b * TB + j - 1))
                    for i in range(j + 1):
                        q = t.matmul((bC, bPT)[b % 2][:, j * P:(j + 1) * P], pT[b % 2][:, i, (j - i) * P:(j - i + 1) * P],
                                     qkv[:, b * TB + i, 2, :], start=(i == 0), stop=(i == j))
                q.then_inc(f_o, 1)

            for b in range(NB):
                output(end, NH, b, b, NH * NB)
                for i in range(TB):
                    n = b * TB + i
                    if n >= 3:
                        pe.wait_ge(f_diag, n - 2)
                        pe.wait_ge(f_rest, rest(n - 3))
                    t.matmul(zq_banks[n % 3][:, 0:SEQ - i * P], zT[:, b, i * P:(i + 1) * P], qT[:, b, i * P:],
                             start=True, stop=True).then_inc(f_p, 1)
                if b:
                    weigh(b - 1)
            weigh(NB - 1)

        @block.scalar
        def _(act):
            for started in (a_cp, c_zE, a_C, a_wo, a_PT):
                act.sem_inc(started, FIRST)
            a = nc.scalar
            act.wait_ge(pro_p, 5)
            a.activation(unused[:, 0:1], ones[:, 0:1], ACT.Sqrt)
            act.wait_ge(wT_mm, 4)
            act.wait_ge(ld_bv, 16)
            a.activation(woT[:], bY[0][:, 3 * P:], ACT.Copy).then_inc(wh_ok, 1)
            a.activation(woTb[:], bY[0][:, 3 * P:], ACT.Copy, scale=bv_c[:, 0:1]).then_inc(wh_ok, 1)
            a.activation(w3h[:, 0:2 * P], bY[0][:, 0:2 * P], ACT.Copy).then_inc(wh_ok, 1)
            a.activation(selh[:], bY[1][:, 0:P], ACT.Copy).then_inc(wh_ok, 1)
            act.wait_ge(wT_mm, 5)
            a.activation(w3h[:, 2 * P:], bG[:, 0:P], ACT.Copy).then_inc(wh_ok, 1)
            a.activation(bias3[:, 2, :], bG[:, P:2 * P], ACT.Copy).then_inc(wh_ok, 1)
            act.wait_ge(var_ok, 1)
            a.activation(small_a[:], rstd[:], ACT.Sqrt).then_inc(root_ok, 1)
            for b in range(NB):
                act.wait_ge(xT_mm, b + 1)
                a.activation(xh[:, b * 512:(b + 1) * 512], bS[b % 2][:], ACT.Copy).then_inc(xh_ok, 1)
            act.wait_ge(kk_ok, 1)
            a.activation(small_b[:], kk[:], ACT.Sqrt).then_inc(kroot_ok, 1)
            act.wait_ge(s_A, 1)
            a.activation(Ah[:], bU[:, 0:P], ACT.Copy, scale=SCALE).then_inc(a_A, 1)
            for b in range(NB):
                act.wait_ge(lg_mm, b + 1)
                a.activation(prob[:, b * TB:(b + 1) * TB, :].rearrange("p a b -> p (a b)"), lg_banks[b][:], ACT.Exp, scale=-1.0).then_inc(lg_ok, 1)
            for n in range(NB):
                act.wait_ge(ut_mm, n + 1)
                a.activation(qT[:, n, :], bS[n % 2][:], ACT.Copy).then_inc(ut_ok, 1)
            act.wait_ge(kn_ok, 1)
            for b in range(NB + 1):
                if b < NB:
                    for k in range(b * TB, (b + 1) * TB):
                        q = a.activation(qkv[:, k, 1, :], qkv[:, k, 1, :], ACT.Copy, scale=kn[:, k:k + 1])
                    q.then_inc(unit_ok, 1)
                if b:
                    act.wait_ge(ut_mm, NB + b)
                    a.activation(uT[:, b - 1, :], bS[(b - 1) % 2][:], ACT.Copy).then_inc(ut_ok, 1)
                if b in (2, 4):
                    act.wait_ge(n_B, b)
                    a.activation(B0[:, b - 2:b, :].rearrange("p b d -> p (b d)"), newton_banks[b // 2 - 1][1][:, 0:2 * P],
                                 ACT.Copy, scale=-1.0).then_inc(n_ev, 1)
            act.wait_ge(ld_v, 16)
            a.activation(vo_h[:, 0, :], vo_raw[:, 0, :], ACT.Copy).then_inc(a_wv, 1)
            act.wait_ge(s_T, 1)
            a.activation(Th[:], bS[0][:], ACT.Copy).then_inc(a_T, 1)
            for n in range(NEWTON):
                for stage in range(2):
                    for c in range(2):
                        act.wait_ge(n_mm, 4 * n + 2 * stage + c + 1)
                        into = (Y0, A[:, 1, :, :])[stage][:, 2 * c:2 * c + 2, :]
                        a.activation(into.rearrange("p b d -> p (b d)"), newton_banks[c][stage][:, 0:2 * P], ACT.Copy).then_inc(n_ev, 1)

            def scaled(plan, turn, n, g, g4, k, side=1):
                act.wait_ge((s_Y0, s_Y1)[g], FIRST + turn * STEPS + n + 1)
                m = plan.act_at(n, g)
                act.wait_ge(p_half, FIRST + turn * head.sums + plan.taken(m - 4))
                for e in range(GH):
                    a.activation(tmp[:, m % 4, e, :], (second_Y(side, n) if g else first_Y[n % 2])[:, e * P:(e + 1) * P], ACT.Copy,
                                 scale=g4[:, k, g * GH + e:g * GH + e + 1]).then_inc(a_cp, 1)

            def output(plan, h, n, b, j, batches):
                if j == 0:
                    act.wait_ge(d_goh, FIRST + batches)
                for g in range(2):
                    if g or not plan.on_dve[n]:
                        scaled(plan, h, n, g, goh[:, b % 2, :, :], j)

            def project(count):
                act.wait_ge(s_T, count)
                a.activation(Th[:], bS[0][:], ACT.Copy).then_inc(a_T, 1)

            act.wait_ge(nil_ok, 5)
            with act.Fori(0, NH) as h:
                def context(b):
                    act.wait_ge(s_PV, FIRST + h * NB * TB + (b + 1) * TB)
                    a.activation(ch[:], bC[:], ACT.Copy).then_inc(a_C, 1)

                act.wait_ge(d_gh, h * 2 + 2)
                for b in range(NB):
                    for i in range(TB):
                        n = h * NB * TB + b * TB + i
                        act.wait_ge(d_max, n + 1)
                        a.activation(prb[:, i, :], bS[i % 2][:], ACT.Exp, bias=nmax[:, b % 2, i:i + 1],
                                     accum_out=rsum[:, b % 2, i:i + 1]).then_inc(a_exp, 1)
                        if b == 0 and i == 1:
                            act.wait_ge(c_au, h + 1)
                            a.activation(uA[:].rearrange("p f d -> p (f d)"), bG[:, 2 * P:], ACT.Copy).then_inc(c_uA, 1)
                        if b == 0 and i == 2:
                            act.wait_ge(c_auT, h + 1)
                            a.activation(AuT[:].rearrange("p f b d -> p (f b d)"), bG[:, 0:2 * P], ACT.Copy).then_inc(c_auE, 1)
                        if i == TB - 1:
                            project(h * NB + b + 2)
                        if b and i == 0:
                            context(b - 1)
                        scaled(head, h, v_at(b, i), 1, gh[:, 0, :, :], b * TB + i, side=0)
                        if b == 1 and i == 0:
                            act.wait_ge(ld_o, h * 16 + 16)
                            act.wait_ge(s_Y1, FIRST + h * STEPS + o_at(0, TB - 1) + 1)
                            a.activation(vo_h[:, 1, :], vo_raw[:, 1, :], ACT.Copy).then_inc(a_wo, 1)
                        if b == NB - 1 and i == 0:
                            act.wait_ge(c_W, h + 1)
                            a.activation(Wc[:].rearrange("p f d -> p (f d)"), bG[:, 2 * P:], ACT.Copy).then_inc(c_WE, 1)
                            for f in range(2):
                                a.activation(Zc[:, f, :], bG[:, 2 * P + f * P:3 * P + f * P], ACT.Copy, scale=rDf[:, f:f + 1]).then_inc(c_WE, 1)
                        if b == NB - 1 and i == 1:
                            act.wait_ge(s_A, h + 2)
                            a.activation(Ah[:], bC[:, 0:P], ACT.Copy, scale=SCALE).then_inc(a_A, 1)
                    for j in range(TB):
                        n = h * NB * TB + b * TB + j
                        act.wait_ge(s_PT, n + 1)
                        if j == 0:
                            act.wait_ge(s_PV, FIRST + h * NB * TB + b * TB)
                        if j >= 2:
                            act.wait_ge(s_PV, FIRST + n - 1)
                        a.activation(pTs[:, j % 2, :], bPT[:], ACT.Copy).then_inc(a_PT, 1)
                        output(head, h, o_at(b, j), (b - 1) % NB, j, h * NB + b)
                        if b == NB - 1 and j == 0:
                            act.wait_ge(ld_v, h * 16 + 32)
                            a.activation(vo_h[:, 0, :], vo_raw[:, 0, :], ACT.Copy).then_inc(a_wv, 1)
                            act.wait_ge(c_z, h + 1)
                            for f in range(2):
                                a.activation(zT[:, :, bass.ds(f * (SEQ // 2) + h * CHUNK, CHUNK)],
                                             bG[:, f * P:(f + 1) * P].rearrange("p (b d) -> p b d", b=NB), ACT.Copy).then_inc(c_zE, 1)
                    if b == NB - 1:
                        context(b)
            for b in range(NB):
                output(end, NH, b, NB - 1, b, NH * NB)
                if b >= 2:
                    act.wait_ge(f_o, b - 1)
                for i in range(TB - 1):
                    act.wait_ge(f_diag, b * TB + i + 1)
                    w = SEQ - i * P
                    a.activation(pT[b % 2][:, i, P:w], zq_banks[(b * TB + i) % 3][:, P:w], ACT.Copy).then_inc(f_rest, 1)

        @block.vector
        def _(dve):
            for started in (d_V, d_gate, d_C, d_goh, c_A):
                dve.sem_inc(started, FIRST)
            v = nc.vector
            linked = [0]

            def link(ins):
                linked[0] += 1
                ins.then_inc(link_ok, 1)
                dve.wait_ge(link_ok, linked[0])

            def wide(g2):
                return g2[:].rearrange("p (g a) -> p g a", a=1).broadcast_to([P, NG, NE])

            def grouped(g3):
                return g3[:].rearrange("p k (g e) -> p (k g) e", e=NE)

            dve.wait_ge(ident_ok, 3)
            for b in range(NB):
                r = slice(b * CHUNK, (b + 1) * CHUNK)
                link(v.tensor_copy(eye32[r, :], ident[r, r]))
                link(v.tensor_copy(nmask[r, :], nlow[r, r]))
            dve.wait_ge(ident_ok, 4)
            link(v.tensor_copy(id2_r[:], id2[:]))
            link(v.tensor_copy(ident_r[:], ident[:]))
            link(v.tensor_reduce(own[:], ident[:].rearrange("p (b k) -> p b k", b=NB), AX_X, ALU.add))
            for k in range(NT):
                dve.wait_ge(ld_x[k // TB], 16)
                q = v.bn_stats(stats[:, k, :], x_sb[:, k, :])
            link(q)
            for k in range(NT):
                q = v.bn_aggr(mv[:, k, :], stats[:, k, :])
            link(q)
            v.tensor_scalar(rstd[:], mv[:, :, 1], LN_EPS, None, ALU.add).then_inc(var_ok, 1)
            dve.wait_ge(root_ok, 1)
            dve.wait_ge(var_ok, 1)
            link(v.reciprocal(small_b[:], small_a[:]))
            link(v.tensor_tensor(small_a[:], small_b[:], small_b[:], ALU.mult))
            link(v.tensor_tensor(small_a[:], small_a[:], rstd[:], ALU.mult))
            link(v.tensor_scalar(small_a[:], small_a[:], -0.5, 1.5, ALU.mult, ALU.add))
            link(v.tensor_tensor(rstd[:], small_a[:], small_b[:], ALU.mult))
            for k in range(NT):
                q = v.tensor_scalar(xn[:, k, :], x_sb[:, k, :], mv[:, k, 0:1], rstd[:, k:k + 1], ALU.subtract, ALU.mult)
                if k % TB == TB - 1:
                    q.then_inc(xn_ok, 1)
            dve.wait_ge(wh_ok, 6)
            v.tensor_tensor(w3l[:, 0:2 * P], bY[0][:, 0:2 * P], w3h[:, 0:2 * P].bitcast(F32), ALU.subtract).then_inc(wl_ok, 1)
            v.tensor_tensor(w3l[:, 2 * P:], bG[:, 0:P], w3h[:, 2 * P:].bitcast(F32), ALU.subtract).then_inc(wl_ok, 1)
            v.tensor_tensor(sell[:], bY[1][:, 0:P], selh[:].bitcast(F32), ALU.subtract).then_inc(wl_ok, 1)
            for b in range(NB):
                dve.wait_ge(xh_ok, b + 1)
                c = slice(b * 512, (b + 1) * 512)
                v.tensor_tensor(xl[:, c], bS[b % 2][:], xh[:, c].bitcast(F32), ALU.subtract).then_inc(xl_ok, 1)
            dve.wait_ge(ld_b, 64)
            for k in range(NT + 1):
                if k < NT:
                    dve.wait_ge(qkv_mm, k + 1)
                    v.tensor_tensor(qkv[:, k, :, :], (bG, bU)[k % 2][:, 0:3 * P].rearrange("p (a b) -> p a b", a=3),
                                    bias3[:], ALU.add).then_inc(qkv_ok, 1)
                if k:
                    dve.wait_ge(qkv_ok, k)
                    q = v.tensor_tensor_reduce(pick[:, k - 1, :], qkv[:, k - 1, 1, :], qkv[:, k - 1, 1, :], 1.0, 0.0, ALU.mult, ALU.add, kk[:, k - 1:k])
                    if k == NT:
                        q.then_inc(kk_ok, 1)
                    q = v.tensor_tensor_reduce(tmpg[:, k - 1, :], qkv[:, k - 1, 0, :], qkv[:, k - 1, 1, :], 1.0, 0.0, ALU.mult, ALU.add, kq[:, k - 1:k])
            q.then_inc(kk_ok, 1)
            dve.wait_ge(kk_ok, 2)
            dve.wait_ge(kroot_ok, 1)
            link(v.tensor_scalar(small_a[:], small_b[:], TINY, None, ALU.max))
            link(v.reciprocal(small_a[:], small_a[:]))
            link(v.tensor_tensor(small_a[:], small_a[:], kk[:], ALU.mult))
            link(v.tensor_tensor(small_a[:], small_a[:], small_b[:], ALU.add))
            link(v.tensor_scalar(small_a[:], small_a[:], 0.5, NORM_EPS, ALU.mult, ALU.add))
            v.reciprocal(kn[:], small_a[:]).then_inc(kn_ok, 1)
            dve.wait_ge(a_A, 1)
            v.scalar_tensor_tensor(out=Al[:], in0=bU[:, 0:P], scalar=SCALE, in1=Ah[:].bitcast(F32),
                                   op0=ALU.mult, op1=ALU.subtract).then_inc(d_A, 1)
            dve.wait_ge(lg_ok, NB)
            dve.wait_ge(zero_ok, NE + 2)
            ranks = rank[:].rearrange("p (a e) -> p a e", a=1).broadcast_to([P, NG, NE])

            def first(least, out_):
                link(v.tensor_tensor(grouped(out_), grouped(out_ if out_ is tmpg else prob), wide(least), ALU.is_equal))
                link(v.tensor_tensor(grouped(out_), grouped(out_), ranks, ALU.mult))
                link(v.tensor_reduce(topr[:], grouped(out_), AX_X, ALU.max))
                link(v.tensor_tensor(grouped(out_), grouped(out_), wide(topr), ALU.is_equal))

            link(v.tensor_scalar(prob[:], prob[:], 1.0, MOST, ALU.add, ALU.min))
            link(v.tensor_reduce(top1[:], grouped(prob), AX_X, ALU.min))
            first(top1, pick)
            link(v.scalar_tensor_tensor(out=tmpg[:], in0=pick[:], scalar=BEYOND, in1=prob[:], op0=ALU.mult, op1=ALU.max))
            link(v.tensor_reduce(top2[:], grouped(tmpg), AX_X, ALU.min))
            first(top2, tmpg)
            link(v.reciprocal(top1[:], top1[:]))
            link(v.reciprocal(top2[:], top2[:]))
            link(v.tensor_tensor(topr[:], top1[:], top2[:], ALU.add))
            link(v.tensor_scalar(topr[:], topr[:], 1e-9, None, ALU.max))
            link(v.reciprocal(topr[:], topr[:]))
            link(v.tensor_scalar(topr[:], topr[:], rs_b[:, 0:1], None, ALU.mult))
            link(v.tensor_tensor(top1[:], top1[:], topr[:], ALU.mult))
            link(v.tensor_tensor(top2[:], top2[:], topr[:], ALU.mult))
            link(v.tensor_tensor(grouped(pick), grouped(pick), wide(top1), ALU.mult))
            link(v.tensor_tensor(grouped(tmpg), grouped(tmpg), wide(top2), ALU.mult))
            link(v.tensor_tensor(gate[:], pick[:], tmpg[:], ALU.add))

            def eliminate(k, parts, part, at):
                if parts == 5:
                    dve.wait_ge(elim_ok, at + part if part < 4 else at + part - 1)
                    stage, fs = min(part, 3), slice(0, 2)
                    halves = (part - 3,)
                else:
                    dve.wait_ge(elim_ok, at + part - 1)
                    stage, fs = part // 2, slice(part % 2, part % 2 + 1)
                    halves = (part % 2,)
                if stage == 0:
                    q = v.stream_shuffle(row[:, fs, :], M[:, fs, k:k + CHUNK + 1], [k] * CHUNK)
                elif stage == 1:
                    q = v.reciprocal(rp[:, fs], row[:, fs, 0])
                elif stage == 2:
                    q = v.scalar_tensor_tensor(out=cf[:, fs], in0=M[:, fs, k], scalar=nmask[:, k:k + 1], in1=rp[:, fs], op0=ALU.mult, op1=ALU.mult)
                else:
                    f = halves[0]
                    w = M[:, f, k + 1:k + CHUNK + 1]
                    q = v.scalar_tensor_tensor(out=w, in0=row[:, f, 1:], scalar=cf[:, f:f + 1], in1=w, op0=ALU.mult, op1=ALU.add)
                q.then_inc(elim_ok, 1)

            def gated(plan, turn, n, into, g4, k, fresh, between):
                dve.wait_ge(s_Y0, FIRST + turn * STEPS + n + 1)
                for e in range(GH):
                    dve.wait_ge(d_gate, FIRST + turn * (GH * head.dve) + GH * plan.dve_at(n) + e)
                    y, g1 = first_Y[n % 2][:, e * P:(e + 1) * P], g4[:, k, e:e + 1]
                    if fresh and e == 0:
                        q = v.tensor_scalar(into, y, g1, None, ALU.mult)
                    else:
                        q = v.scalar_tensor_tensor(out=into, in0=y, scalar=g1, in1=into, op0=ALU.mult, op1=ALU.add)
                    q.then_inc(d_gate, 1)
                    for part in between[e:e + 1] if e < GH - 1 else between[e:]:
                        eliminate(*part)

            def project(count):
                dve.wait_ge(a_T, count)
                v.tensor_tensor(Tl[:], bS[0][:], Th[:].bitcast(F32), ALU.subtract).then_inc(d_T, 1)

            project(1)
            dve.wait_ge(acc_ok, 1)
            dve.wait_ge(nil_ok, 5)
            with dve.Fori(0, NH) as h:
                dve.sem_clear(elim_ok)

                def build():
                    dve.wait_ge(c_g, FIRST + h + 1)
                    v.tensor_tensor(M[:, :, 0:CHUNK], bG[:, 0:2 * CHUNK].rearrange("p (f k) -> p f k", f=2),
                                    eye32[:].rearrange("p (a k) -> p a k", a=1).broadcast_to([P, 2, CHUNK]), ALU.add).then_inc(elim_ok, 1)
                    v.tensor_copy(M[:, :, CHUNK:], eye32[:].rearrange("p (a k) -> p a k", a=1).broadcast_to([P, 2, CHUNK])).then_inc(elim_ok, 1)

                def finish_factor():
                    at = ELIMINATED
                    dve.wait_ge(elim_ok, at)
                    for f in range(2):
                        if f:
                            dve.wait_ge(elim_ok, at + f)
                        v.tensor_tensor_reduce(scr32[:], M[:, f, 0:CHUNK], eye32[:], 1.0, 0.0, ALU.mult, ALU.add, Dv[:, f:f + 1]).then_inc(elim_ok, 1)
                    for f in range(2):
                        for b in range(NB):
                            r = slice(b * CHUNK, (b + 1) * CHUNK)
                            v.transpose(Rbd[r, f, r], M[r, f, CHUNK:]).then_inc(elim_ok, 1)
                    dve.wait_ge(elim_ok, at + 2)
                    v.reciprocal(rDf[:], Dv[:]).then_inc(c_fac, 1)

                def output(b, j, n, between):
                    if head.on_dve[n]:
                        if j == 0:
                            dve.wait_ge(d_goh, FIRST + h * NB + b)
                        gated(head, h, n, acc[:, (b - 1) % NB * TB + j, :], goh[:, (b - 1) % 2, :, :], j, False, between)
                    else:
                        for part in between:
                            eliminate(*part)

                def context(b):
                    dve.wait_ge(a_C, FIRST + h * NB + b + 1)
                    v.tensor_tensor(cl[:], bC[:], ch[:].bitcast(F32), ALU.subtract).then_inc(d_C, 1)

                dve.wait_ge(c_g, FIRST + h)
                v.tensor_copy(uTc[:].rearrange("p f b k -> p b f k"),
                              uT[:].rearrange("p b (f k) -> p b f k", f=2)[:, :, :, bass.ds(h * CHUNK, CHUNK)]).then_inc(c_uT, 1)
                dve.wait_ge(a_cp, FIRST + h * (GH * head.act) + GH * (head.act_at(v_at(NB - 1, TB - 1), 1) + 1 - head.act))
                dve.wait_ge(d_goh, FIRST + h * NB)
                v.tensor_copy(gh[:, 0, :, :], gate[:, :, bass.ds(h * NE, NE)]).then_inc(d_gh, 1)
                v.tensor_copy(gh[:, 1, :, :], gate[:, :, bass.ds(NH * NE + h * NE, NE)]).then_inc(d_gh, 1)
                dve.wait_ge(d_gh, h * 2 + 2)
                for b in range(NB):
                    def largest(i):
                        dve.wait_ge(s_S, h * NB * TB + b * TB + i + 1)
                        v.tensor_reduce(nmax[:, b % 2, i:i + 1], bS[i % 2][:], AX_X, ALU.max, negate=True).then_inc(d_max, 1)

                    largest(0)
                    for i in range(TB):
                        ph = v_at(b, i)
                        if i < TB - 1:
                            largest(i + 1)
                        if ph == BUILD_AT:
                            build()
                        gated(head, h, ph, Va[:, i, :], gh[:, 0, :, :], b * TB + i, True, PARTS_OF[ph])
                        if b and i == 0:
                            context(b - 1)
                        if ph == UPDATE_AT + 1:
                            dve.wait_ge(a_A, h + 2)
                            v.scalar_tensor_tensor(out=Al[:], in0=bC[:, 0:P], scalar=SCALE, in1=Ah[:].bitcast(F32),
                                                   op0=ALU.mult, op1=ALU.subtract).then_inc(d_A, 1)

                    def values():
                        dve.wait_ge(p_quart, FIRST + h * STEPS + v_at(b, TB - 1) + 1)
                        dve.wait_ge(d_gate, FIRST + h * (GH * head.dve) + GH * head.dve_at(v_at(b, TB - 1) + 1))
                        dve.wait_ge(s_PV, FIRST + h * (NB * TB) + b * TB)
                        v.tensor_tensor(Vs[:], Va[:], Vb[:], ALU.add).then_inc(d_V, 1)
                        dve.wait_ge(a_exp, h * NB * TB + (b + 1) * TB)
                        v.reciprocal(rinv[:], rsum[:, b % 2, :]).then_inc(d_rinv, 1)
                        dve.wait_ge(a_cp, FIRST + h * (GH * head.act) + GH * (head.act_at(o_at(b - 1, TB - 1), 1) + 1 if b else
                                                                              head.act_at(o_at(NB - 1, TB - 1), 1) + 1 - head.act))
                        dve.wait_ge(d_rinv, h * NB + b + 1)
                        v.tensor_tensor(goh[:, b % 2, :, :], gh[:, 1, b * TB:(b + 1) * TB, :],
                                        rinv[:].rearrange("p (k a) -> p k a", a=1).broadcast_to([P, TB, NE]), ALU.mult).then_inc(d_goh, 1)

                    def update(f):
                        dve.wait_ge(c_up, h * 2 + f + 1)
                        v.tensor_tensor(A[:, f, :, :].rearrange("p b d -> p (b d)"), A[:, f, :, :].rearrange("p b d -> p (b d)"),
                                        (bPT, bC)[f][:], ALU.subtract).then_inc(c_A, 1)

                    if b == NB - 1:
                        update(0)
                    project(h * NB + b + 2)
                    if b == NB - 1:
                        update(1)
                    if not head.on_dve[o_at(b, 0)]:
                        values()
                    for j in range(TB):
                        ph = o_at(b, j)
                        if j == 0 and head.on_dve[ph]:
                            output(b, j, ph, PARTS_OF[ph][:GH - 1])
                            values()
                            for part in PARTS_OF[ph][GH - 1:]:
                                eliminate(*part)
                        else:
                            output(b, j, ph, PARTS_OF[ph])
                        if ph == FACTORED:
                            finish_factor()
                    if b == NB - 1:
                        context(b)
            dve.wait_ge(d_goh, FIRST + NH * NB)
            dve.wait_ge(d_gh, NH * 2)

            def both_sums(b):
                k = slice(b * TB, (b + 1) * TB)
                dve.wait_ge(p_acc, FIRST + NH * NB * TB + (TB if b == NB - 1 else 0))
                dve.wait_ge(d_gate, FIRST + NH * GH * head.dve + GH * (b + 1))
                v.tensor_tensor(acc[:, k, :], acc[:, k, :], acc2[:, k, :], ALU.add).then_inc(f_sum, 1)

            def result(b):
                k = slice(b * TB, (b + 1) * TB)
                dve.wait_ge(f_sum, b + 1)
                dve.wait_ge(f_o, b + 1)
                v.tensor_tensor(acc[:, k, :].rearrange("p k d -> p (k d)"), acc[:, k, :].rearrange("p k d -> p (k d)"),
                                (bC, bPT)[b % 2][:], ALU.add).then_inc(f_res, 1)

            for b in range(NB):
                gated(end, NH, b, acc[:, (NB - 1) * TB + b, :], goh[:, (NB - 1) % 2, :, :], b, False, [])
                if b >= 2:
                    dve.wait_ge(f_o, b - 1)
                for i in range(TB):
                    n = b * TB + i
                    dve.wait_ge(f_p, n + 1)
                    v.tensor_tensor(pT[b % 2][:, i, 0:P], zq_banks[n % 3][:, 0:P], causal[:], ALU.mult).then_inc(f_diag, 1)
                both_sums(b)
                if b:
                    result(b - 1)
            result(NB - 1)


_INS = ['L0_attn_x', 'L0_attn_Wq', 'L0_attn_bq', 'L0_attn_Wk', 'L0_attn_bk', 'L0_attn_Wv', 'L0_attn_bv', 'L0_attn_Wo', 'L0_attn_bo',
        'L0_ffn_q_w', 'L0_ffn_k_w', 'L0_ffn_v_w', 'L0_ffn_o_w', 'L0_ffn_sel_v_w', 'L0_ffn_sel_o_w', 'L0_ffn_route_scale']


def kernel(**inputs):
    import numpy as np
    import concourse.bacc as bacc
    from concourse.bass_utils import run_bass_kernel_spmd

    nc = bacc.Bacc("TRN2", target_bir_lowering=False, num_devices=1)
    arrays, args = {}, []
    for name in _INS:
        a = np.ascontiguousarray(inputs[name])
        arrays[name] = a
        args.append(nc.dram_tensor(name, a.shape, mybir.dt.from_np(a.dtype), kind="ExternalInput").ap())
    shape = inputs['L0_attn_x'].shape
    out = nc.dram_tensor("out", shape, F32, kind="ExternalOutput").ap()
    block_kernel(nc, *args, out)
    r = run_bass_kernel_spmd(nc, [arrays], core_ids=[0])
    return r.results[0]["out"]
```
